# Optimizing a Trainium2 kernel written in Bass

```python
import numpy as np
import jax
import jax.numpy as jnp

def _softmax(x, axis=-1):
    return jax.nn.softmax(x, axis=axis)

def _gelu(x):
    return jax.nn.gelu(x, approximate=True)

def _silu(x):
    return jax.nn.silu(x)

def _sigmoid(x):
    return jax.nn.sigmoid(x)

def _layernorm(x, axis=-1, eps=1e-05):
    m = jnp.mean(x, axis=axis, keepdims=True)
    v = jnp.var(x, axis=axis, keepdims=True)
    return (x - m) / jnp.sqrt(v + eps)

def _scatter_add(tgt, idx, src, axis=0):
    return tgt.at[idx].add(src)

def _segment_sum(src, seg, n):
    return jax.ops.segment_sum(src, seg, n)
kernel_name = 'mk_seq_preln_d1_jaxref_r4_a30834'

def setup_inputs(seed: int=0):
    np.random.seed(seed)
    _w = jnp.asarray

    def _L0_attn_setup():
        import jax, jax.numpy as jnp
        import numpy as np
        INF_APPROX = 1e+30
        ROTARY_BASE = 10000.0
        D_HEAD = 128

        def _rope(x, base=ROTARY_BASE):
            _, length, _, width = x.shape
            half = width // 2
            positions = jnp.arange(length, dtype=x.dtype)
            dims = jnp.arange(half, dtype=x.dtype)
            ang_freqs = jnp.power(base, -dims / half)
            radians = positions[:, None] * ang_freqs[None, :]
            cos = jnp.cos(radians)[None, :, None, :]
            sin = jnp.sin(radians)[None, :, None, :]
            even, odd = jnp.split(x, 2, axis=-1)
            return jnp.concatenate([even * cos - odd * sin, even * sin + odd * cos], axis=-1)
        key = jax.random.key(seed)
        k1, k2, k3, k4, k5 = jax.random.split(key, 5)
        B, T, M, H, D = (2, 1024, 256, 8, 128)
        n_layer = 24
        x = jax.random.normal(k1, (B, T, M), dtype=jnp.float32)
        std_qkv = M ** (-0.5)
        std_o = (M * 2 * n_layer) ** (-0.5)
        w_aq = jnp.zeros((M, H, D), dtype=jnp.float32)
        w_ak = std_qkv * jax.random.normal(k3, (M, H, D), dtype=jnp.float32)
        w_av = std_qkv * jax.random.normal(k4, (M, H, D), dtype=jnp.float32)
        w_ao = std_o * jax.random.normal(k5, (H, D, M), dtype=jnp.float32)
        return {'x': x, 'w_aq': w_aq, 'w_ak': w_ak, 'w_av': w_av, 'w_ao': w_ao}
    _L0_attn_in = _L0_attn_setup()

    def _L0_ffn_setup():
        import jax, jax.numpy as jnp
        import numpy as np
        E, D, F = (8, 256, 1024)
        B, S = (4, 512)

        def _layernorm(x, g, b, eps=1e-05):
            mu = jnp.mean(x, axis=-1, keepdims=True)
            var = jnp.var(x, axis=-1, keepdims=True)
            return (x - mu) * jax.lax.rsqrt(var + eps) * g + b
        key = jax.random.key(seed)
        ks = jax.random.split(key, 5)
        return {'input_features': jax.random.normal(ks[0], (B, S, D), jnp.float32), 'centroids': jax.random.normal(ks[1], (E, D), jnp.float32) * 0.1, 'ln_g': jnp.ones((E, D), jnp.float32), 'ln_b': jnp.zeros((E, D), jnp.float32), 'w1': jax.random.normal(ks[2], (E, F, D), jnp.float32) * (1.0 / np.sqrt(D).astype(np.float32)), 'b1': jnp.zeros((E, F), jnp.float32), 'w2': jax.random.normal(ks[3], (E, D, F), jnp.float32) * (1.0 / np.sqrt(F).astype(np.float32)), 'b2': jnp.zeros((E, D), jnp.float32)}
    _L0_ffn_in = _L0_ffn_setup()
    _d = {'L0_attn_x': _L0_attn_in['x'], 'L0_attn_w_aq': _L0_attn_in['w_aq'], 'L0_attn_w_ak': _L0_attn_in['w_ak'], 'L0_attn_w_av': _L0_attn_in['w_av'], 'L0_attn_w_ao': _L0_attn_in['w_ao'], 'L0_ffn_centroids': _L0_ffn_in['centroids'], 'L0_ffn_ln_g': _L0_ffn_in['ln_g'], 'L0_ffn_ln_b': _L0_ffn_in['ln_b'], 'L0_ffn_w1': _L0_ffn_in['w1'], 'L0_ffn_b1': _L0_ffn_in['b1'], 'L0_ffn_w2': _L0_ffn_in['w2'], 'L0_ffn_b2': _L0_ffn_in['b2']}
    _x0 = _d['L0_attn_x']
    _d['L0_attn_x'] = jax.random.normal(jax.random.fold_in(jax.random.key(seed), 1), (8, 512, 256), dtype=_x0.dtype)
    del _x0
    return _d

def reference(L0_attn_x, L0_attn_w_aq, L0_attn_w_ak, L0_attn_w_av, L0_attn_w_ao, L0_ffn_centroids, L0_ffn_ln_g, L0_ffn_ln_b, L0_ffn_w1, L0_ffn_b1, L0_ffn_w2, L0_ffn_b2):

    def _L0_attn_ref(x, w_aq, w_ak, w_av, w_ao):
        import jax, jax.numpy as jnp
        import numpy as np
        INF_APPROX = 1e+30
        ROTARY_BASE = 10000.0
        D_HEAD = 128

        def _rope(x, base=ROTARY_BASE):
            _, length, _, width = x.shape
            half = width // 2
            positions = jnp.arange(length, dtype=x.dtype)
            dims = jnp.arange(half, dtype=x.dtype)
            ang_freqs = jnp.power(base, -dims / half)
            radians = positions[:, None] * ang_freqs[None, :]
            cos = jnp.cos(radians)[None, :, None, :]
            sin = jnp.sin(radians)[None, :, None, :]
            even, odd = jnp.split(x, 2, axis=-1)
            return jnp.concatenate([even * cos - odd * sin, even * sin + odd * cos], axis=-1)
        B, T, M = x.shape
        q = jnp.einsum('btm,mhd->bthd', x, w_aq)
        k = jnp.einsum('btm,mhd->bthd', x, w_ak)
        v = jnp.einsum('btm,mhd->bthd', x, w_av)
        q = _rope(q)
        k = _rope(k)
        s = jnp.einsum('bihd,bjhd->bhij', q, k) / D_HEAD
        i = jnp.arange(T)[:, None]
        j = jnp.arange(T)[None, :]
        mask = (i < j).astype(x.dtype)[None, None, :, :]
        s = s - jnp.asarray(INF_APPROX, x.dtype) * mask
        p = jax.nn.softmax(s, axis=-1)
        o = jnp.einsum('bhij,bjhd->bihd', p, v)
        r = jnp.einsum('bihd,hdm->bim', o, w_ao)
        return r

    def _L0_ffn_ref(input_features, centroids, ln_g, ln_b, w1, b1, w2, b2):
        import jax, jax.numpy as jnp
        import numpy as np
        E, D, F = (8, 256, 1024)
        B, S = (4, 512)

        def _layernorm(x, g, b, eps=1e-05):
            mu = jnp.mean(x, axis=-1, keepdims=True)
            var = jnp.var(x, axis=-1, keepdims=True)
            return (x - mu) * jax.lax.rsqrt(var + eps) * g + b
        Bf, Sf, Df = input_features.shape
        x = input_features.reshape(-1, Df)
        aff = x @ centroids.T
        assign = jnp.argmax(aff, axis=1)
        order = jnp.argsort(assign)
        xs = x[order]
        es = assign[order]
        alpha = jax.nn.sigmoid(jnp.take_along_axis(aff[order], es[:, None], axis=1))
        nE = centroids.shape[0]
        y = jnp.zeros_like(xs)
        for e in range(nE):
            h = _layernorm(xs, ln_g[e], ln_b[e])
            h = jax.nn.relu(h @ w1[e].T + b1[e])
            ye = xs + h @ w2[e].T + b2[e]
            y = y + jnp.where((es == e)[:, None], ye, 0.0)
        out_sorted = alpha * y + (1.0 - alpha) * xs
        inv = jnp.argsort(order)
        return out_sorted[inv].reshape(Bf, Sf, Df)
    x = L0_attn_x
    x = x + _L0_attn_ref(_layernorm(x, axis=-1), L0_attn_w_aq, L0_attn_w_ak, L0_attn_w_av, L0_attn_w_ao)
    x = x + _L0_ffn_ref(_layernorm(x, axis=-1), L0_ffn_centroids, L0_ffn_ln_g, L0_ffn_ln_b, L0_ffn_w1, L0_ffn_b1, L0_ffn_w2, L0_ffn_b2)
    return x

_drawn_inputs = setup_inputs


def setup_inputs(seed=0):
    import zlib

    import numpy as np

    out = dict(_drawn_inputs(seed))
    spreads = {'L0_attn_w_aq': (0.0, 0.44),
     'L0_ffn_ln_g': (1.0, 0.2),
     'L0_ffn_ln_b': (0.0, 0.271),
     'L0_ffn_b1': (0.0, 0.268),
     'L0_ffn_b2': (0.0, 0.1)}
    factors = {'L0_attn_w_ak': 3.17}
    for name, (base, spread) in spreads.items():
        noise = np.random.default_rng([zlib.crc32(name.encode()), seed]).standard_normal(out[name].shape)
        drawn = base * np.exp(spread * noise) if base else spread * noise
        out[name] = jnp.asarray(drawn.astype(out[name].dtype))
    for name, factor in factors.items():
        out[name] = (out[name] * factor).astype(out[name].dtype)
    return out
```

```python
from contextlib import ExitStack

import concourse.bass as bass
from concourse import mybir

F32 = mybir.dt.float32
F32R = mybir.dt.float32r
BF16 = mybir.dt.bfloat16
I32 = mybir.dt.int32
U32 = mybir.dt.uint32
ACT = mybir.ActivationFunctionType
ALU = mybir.AluOpType
AX = mybir.AxisListType

P = 128
EPS = 1e-5
B, T, D = 8, 512, 256
H, DH = 8, 128
E, F = 8, 1024
NI = T // P
KC = D // P
FC = F // P
NT = B * NI
NS = NT + E - 1
G = 4
ROW = 2 * D + 4
POFF = [0, 128, 384, 768]
TOFF = [0, 512, 896, 1152]
CAUSAL = NI * (NI + 1) // 2 * P

C_COSQ, C_SINQ = 0, 256
C_COSK, C_SINK = 768, 1024
C_IOTA = 1536
C_TOK = C_IOTA + P
C_ID = C_TOK + NT
C_MASK = C_ID + P
C_LT = C_MASK + P
C_END = C_LT + P


def build(nc, x, w_q, w_k, w_v, w_o, cent_t, ln_g, ln_b, w1_t, b1, w2_t, b2, consts, out, tok_rows):
    ctx = ExitStack()
    with ctx:
        sem = lambda n: ctx.enter_context(nc.semaphore(n))

        base = (nc.sbuf_base + 63) // 64 * 64
        place = [base]
        size = {F32: 4, F32R: 4, BF16: 2, I32: 4, U32: 4}

        def sb(name, shape, dt):
            n = size[dt]
            for s in shape[1:]:
                n *= s
            t = nc.alloc_sbuf_tensor_at(name, shape, dt, offset=place[0])
            place[0] += (n + 31) // 32 * 32
            assert place[0] <= nc.sbuf_usable_end, (name, place[0])
            return t

        onehot = sb("onehot", [P, NT, E], BF16)
        cst = sb("cst", [P, C_END], F32)
        ident = cst[:, C_ID:C_ID + P]
        ident_b = sb("ident_b", [P, P], BF16)
        mask_b = sb("mask_b", [P, P], BF16)
        lower_b = sb("lower_b", [P, P], BF16)
        ones_b = sb("ones_b", [P, P], BF16)
        cent = sb("cent", [P, KC, E], F32)
        slot_hi = sb("slot_hi", [P, NT], F32)
        slot_lo = sb("slot_lo", [P, NT], F32)
        slot_tok = sb("slot_tok", [P, NS], U32)
        tok_now = sb("tok_now", [P, 6], U32)
        tile_exp = sb("tile_exp", [P, NS], I32)
        ones_f = sb("ones_f", [P, E * NT], F32)
        common_end = place[0]

        xa = sb("xa", [P, NI, D], F32)
        xh = sb("xh", [P, NI, D], F32)
        xth = sb("xth", [P, KC, T], F32R)
        xtl = sb("xtl", [P, KC, T], F32R)
        wh = sb("wh", [P, 3, KC, H * DH], F32R)
        wl = sb("wl", [P, 3, KC, H * DH], F32R)
        qk_at = place[0]
        qkt = sb("qkt", [P, 2, 2, G, T], F32)
        w_raw = nc.alloc_sbuf_tensor_at("w_raw", [P, 3, KC, H * DH], F32, offset=qk_at)
        wo = sb("wo", [P, H, D], F32)
        v = sb("v", [P, NI, H * DH], F32)
        xr = sb("xr", [P, NI, D], F32)
        prob = sb("prob", [P, 2, CAUSAL], F32)
        probt = sb("probt", [P, 2, CAUSAL], F32)
        ot = sb("ot", [P, H, T], F32)
        rope_at = place[0]
        rope_c = sb("rope_c", [P, 2, T], F32)
        rope_s = sb("rope_s", [P, 2, T], F32)
        rope = sb("rope", [P, 2, T], F32)
        rope_end = place[0]
        x1 = sb("x1", [P, NI, D], F32)
        xn = sb("xn", [P, NI, D], F32)
        xnt = sb("xnt", [P, KC, T], F32)
        rows = sb("rows", [P, NI, ROW], F32)
        negmax = sb("negmax", [P, 2, NI], F32)
        denom = sb("denom", [P, 2, NI], F32)
        rdenom = sb("rdenom", [P, 2, NI], F32)
        stats = [sb(f"stats{k}", [P, NI, 6], F32) for k in range(3)]
        mv = [sb(f"mv{k}", [P, NI, 2], F32) for k in range(3)]
        veps = [sb(f"veps{k}", [P, NI], F32) for k in range(3)]
        rstd = [sb(f"rstd{k}", [P, NI], F32) for k in range(3)]
        zero_row = sb("zero_row", [1, ROW], F32)
        mhalf = sb("mhalf", [P, NI], F32)
        aff = sb("aff", [P, NI, E], F32)
        top = sb("top", [P, NI, 8], F32)
        topi = sb("topi", [P, NI, 8], U32)
        topf = sb("topf", [P, NI], F32)
        ealpha = sb("ealpha", [P, NI], F32)
        ealpha1 = sb("ealpha1", [P, NI], F32)
        attn_end = place[0]

        place[0] = common_end
        b2_all = sb("b2_all", [P, E, D], F32)
        b1_col = sb("b1_col", [P, E, FC], F32)
        g_col = sb("g_col", [P, E, KC], F32)
        b_col = sb("b_col", [P, E, KC], F32)
        w12 = sb("w12", [P, E, KC * F + FC * D], F32)
        row_in = sb("row_in", [P, 6, ROW], F32)
        row_out = sb("row_out", [P, 3, D], F32)
        ht = sb("ht", [P, 2, KC, P], F32)
        h1 = sb("h1", [P, 2, F], F32)
        h1t = sb("h1t", [P, 2, FC, P], F32)
        yb = sb("yb", [P, 2, D], F32)
        ffn_end = place[0]
        place[0] = rope_at
        tot = sb("tot", [P, E, NT], F32)
        cum = sb("cum", [P, E, NT], F32)
        cnt = sb("cnt", [P, E], F32)
        cnt_i = sb("cnt_i", [P, E], I32)
        tiles_i = sb("tiles_i", [P, E], I32)
        tiles_f = sb("tiles_f", [P, E], F32)
        tiles_cum = sb("tiles_cum", [P, E], F32)
        adj = sb("adj", [P, E], F32)
        adj2 = sb("adj2", [P, E], F32)
        pos = sb("pos", [P, NT, E], F32)
        slot = sb("slot", [P, NT], F32)
        slot_i = sb("slot_i", [P, NT], I32)
        hi_i = sb("hi_i", [P, NT], I32)
        lo_i = sb("lo_i", [P, NT], I32)
        below = sb("below", [P, NS, E], F32)
        below_n = sb("below_n", [P, NS], F32)
        hot_lo = sb("hot_lo", [P, 8, P], F32)
        hot_hi = sb("hot_hi", [P, 8, NS], F32)

        assert place[0] <= rope_end
        bank = [ctx.enter_context(nc.psum_tensor(f"bank{n}", [P, 512], F32)) for n in range(8)]
        PP = bank[0:2]
        TB = bank[2]
        SB = bank[3:5]
        PT = bank[5:7]
        OB = bank[7]
        FZ, FH, FT, FY = bank[0], bank[1:3], bank[3:5], bank[5:7]

        s_const = sem("const_loaded")
        s_wraw = sem("w_raw_loaded")
        s_wsmall = sem("w_small_loaded")
        s_whead = sem("w_head_made")
        s_wrest = sem("w_rest_made")
        s_cb = sem("bf16_consts_made")
        s_xa = sem("xa_loaded")
        s_xr = sem("xr_loaded")
        s_xmean = sem("x_stats_made")
        s_xrstd = sem("x_rstd_made")
        s_xveps = sem("x_veps_made")
        s_xh = sem("xh_made")
        s_ppdone = sem("pp_written")
        s_ppdve = sem("pp_read_by_dve")
        s_ppact = sem("pp_read_by_act")
        s_xth = sem("xt_head_made")
        s_rope = sem("rope_summed")
        s_tbdone = sem("tb_written")
        s_tbread = sem("tb_read")
        s_score = sem("scores_written")
        s_max = sem("max_made")
        s_exp = sem("exp_made")
        s_rden = sem("rdenom_made")
        s_pscaled = sem("probs_scaled")
        s_ptdone = sem("pt_written")
        s_ptact = sem("pt_read_by_act")
        s_ptdve = sem("pt_read_by_dve")
        s_pv = sem("pv_written")
        s_oread = sem("o_read")
        s_dve = sem("dve_step")
        s_own = [sem(n) for n in ("x_bn_made", "x1_bn_made", "xn_bn_made", "top_index_made", "top_float_made",
                                  "exp_plus_one_made")]
        s_nstat = sem("x1_stats_made")
        s_nveps = sem("x1_veps_made")
        s_nrstd = sem("x1_rstd_made")
        s_xn = sem("xn_made")
        s_zstat = sem("xn_stats_made")
        s_zveps = sem("xn_veps_made")
        s_zrstd = sem("xn_rstd_made")
        s_skip = sem("skip_made")
        s_z = sem("z_made")
        s_top = sem("top_made")
        s_ea = sem("exp_neg_top_made")
        s_gate = sem("gate_made")
        s_rows = sem("rows_stored")
        s_zrow = sem("zero_row_made")
        s_half = sem("mhalf_made")

        s_hot = sem("onehots_made")
        s_count = sem("counts_written")
        s_hhi = sem("slot_tile_hot_made")
        s_route = sem("slot_hot_made")
        s_routeb = sem("slot_hot_used")
        s_ids = sem("slot_tok_written")
        s_idx = sem("slot_tok_made")
        s_texp = sem("tile_exp_made")

        s_fw = sem("ffn_weights_loaded")
        s_gat = [sem(f"row_gathered{k}") for k in range(6)]
        s_sca = [sem(f"row_scattered{k}") for k in range(3)]
        s_passed = sem("wait_passed")
        s_now = sem("tok_now_made")
        s_zt = sem("zt_written")
        s_ht = sem("ht_made")
        s_h1 = sem("h1_written")
        s_h1a = sem("h1_read_by_act")
        s_h1d = sem("h1_read_by_dve")
        s_hT = sem("h1t_written")
        s_hTa = sem("h1t_read_by_act")
        s_hTd = sem("h1t_read_by_dve")
        s_y = sem("y_written")
        s_yb = sem("y_biased")
        s_comb = sem("row_combined")

        DVE0 = lambda b: 10 + 22 * b
        ACT0 = lambda b: 8 + 8 * b
        PPN = lambda b: 18 + 30 * b
        UN = lambda b: 8 + 16 * b
        tbn = lambda b, first: 8 if first else 5 + 19 * b

        x_v = x.rearrange("b (i p) d -> b p i d", p=P)
        rows_v = tok_rows[0:B * T, :].rearrange("(b i p) r -> b p i r", p=P, i=NI)
        out_v = out.rearrange("b t d -> (b t) d")

        block = ctx.enter_context(nc.Block())

        def passed(eng):
            eng.sem_inc(s_passed, 1)

        @block.sync
        def _(sp):
            sp.dma_start(cst[:, :], consts).then_inc(s_const, 16)
            sp.dma_start(xa[:, :, :], x_v[0]).then_inc(s_xa, 16)
            for n, w in ((0, w_q), (1, w_k), (2, w_v)):
                sp.dma_start(w_raw[:, n, :, :], w.rearrange("(c p) n -> p c n", p=P)).then_inc(s_wraw, 16)
            sp.dma_start(wo[:, :, :], w_o.rearrange("(h p) n -> p h n", p=P)).then_inc(s_wsmall, 16)
            sp.dma_start(cent[:, :, :], cent_t.rearrange("(c p) e -> p c e", p=P)).then_inc(s_wsmall, 16)
            sp.dma_start(xr[:, :, :], x_v[0]).then_inc(s_xr, 16)
            sp.wait_ge(s_xh, 1)
            sp.dma_start(xa[:, :, :], x_v[1]).then_inc(s_xa, 16)
            sp.wait_ge(s_zrow, 1)
            sp.dma_start(tok_rows[B * T:B * T + 1, :], zero_row[:, :]).then_inc(s_rows, 16)
            sp.wait_ge(s_rows, 16)

            def store_rows(b):
                sp.wait_ge(s_z, 1 * (b + 1))
                sp.wait_ge(s_skip, 1 * (b + 1))
                sp.wait_ge(s_gate, 1 * (b + 1))
                sp.dma_start(rows_v[bass.ds(b, 1)].rearrange("o p i r -> (o p) i r"),
                             rows[:, :, :]).then_inc(s_rows, 16)

            def load_xr(b):
                sp.wait_ge(s_ppdve, DVE0(b))
                sp.dma_start(xr[:, :, :], x_v[bass.ds(b, 1)].rearrange("o p i d -> (o p) i d")).then_inc(s_xr, 16)

            def load_xa(b):
                sp.wait_ge(s_xh, b)
                sp.dma_start(xa[:, :, :], x_v[bass.ds(b, 1)].rearrange("o p i d -> (o p) i d")).then_inc(s_xa, 16)

            with sp.Fori(1, B - 1) as b:
                load_xa(b + 1)
                load_xr(b)
                store_rows(b - 1)
            load_xr(B - 1)

            def load_expert(e):
                sp.dma_start(w12[:, e, 0:KC * F].rearrange("p (c f) -> p c f", c=KC),
                             w1_t[e].rearrange("(c p) f -> p c f", p=P)).then_inc(s_fw, 16)
                sp.dma_start(w12[:, e, KC * F:KC * F + FC * D].rearrange("p (c d) -> p c d", c=FC),
                             w2_t[e].rearrange("(c p) d -> p c d", p=P)).then_inc(s_fw, 16)

            sp.wait_ge(s_ppdone, PPN(B - 1) + 8)
            for t, src in ((g_col, ln_g), (b_col, ln_b)):
                sp.dma_start(t[:, :, :], src.rearrange("e (c p) -> p e c", p=P),
                             allow_slow_non_contiguous=True).then_inc(s_fw, 16)
            sp.dma_start(b1_col[:, :, :], b1.rearrange("e (c p) -> p e c", p=P),
                         allow_slow_non_contiguous=True).then_inc(s_fw, 16)
            sp.dma_start(b2_all[:, :, :].rearrange("p e d -> p (e d)"),
                         b2.rearrange("e d -> (e d)").rearrange("(o n) -> o n", o=1).broadcast_to([P, E * D])
                         ).then_inc(s_fw, 16)
            for e in range(3):
                load_expert(e)
            sp.wait_ge(s_score, 32 * (B - 1) + 16)
            load_expert(3)
            store_rows(B - 2)
            sp.wait_ge(s_score, 32 * B)
            load_expert(4)
            sp.wait_ge(s_ppdve, DVE0(B - 1) + 12)
            load_expert(5)
            load_expert(6)
            load_expert(7)
            store_rows(B - 1)

        FW = 16 * (4 + 2 * E)

        @block.gpsimd
        def _(pool):
            pool.memset(mhalf[:, :], -0.5).then_inc(s_half, 1)
            pool.memset(ones_b[:, :], 1.0).then_inc(s_cb, 1)
            pool.memset(ones_f[:, :], 1.0).then_inc(s_cb, 1)
            pool.memset(zero_row[:, :], 0.0).then_inc(s_zrow, 1)
            pool.memset(rows[:, :, 2 * D + 1:ROW], 0.0).then_inc(s_half, 1)
            pool.wait_ge(s_half, 2)

            def power(k, stat, made, done, n):
                pool.wait_ge(stat, n + 1)
                passed(pool)
                pool.tensor_scalar(veps[k][:, :], mv[k][:, :, 1], EPS, None, ALU.add).then_inc(made, 1)
                pool.wait_ge(made, n + 1)
                pool.tensor_tensor(rstd[k][:, :], veps[k][:, :], mhalf[:, :], ALU.pow).then_inc(done, 1)

            def rope_sum(u, ready):
                pool.wait_ge(s_ppdve, ready)
                pool.tensor_tensor(rope[:, u % 2, :], rope_c[:, u % 2, :], rope_s[:, u % 2, :],
                                   ALU.add).then_inc(s_rope, 1)

            def skip(b):
                pool.wait_ge(s_xn, b + 1)
                pool.wait_ge(s_rows, 16 * (b + 1))
                pool.tensor_tensor(rows[:, :, D:2 * D], x1[:, :, :], xn[:, :, :], ALU.add).then_inc(s_skip, 1)

            def batch(b, first=False, last=False):
                for h in range(H):
                    if h == 1 and not last:
                        power(0, s_xmean, s_xveps, s_xrstd, b + 1)
                    if h < 4 or not last:
                        at = DVE0(b) + 2 * h + (0 if h < 4 else 2)
                        rope_sum(2 * h + 8, at + 1)
                        rope_sum(2 * h + 9, at + 2)
                    if h == 1 and not first:
                        skip(b - 1)
                power(1, s_nstat, s_nveps, s_nrstd, b)
                power(2, s_zstat, s_zveps, s_zrstd, b)

            power(0, s_xmean, s_xveps, s_xrstd, 0)
            for u in range(8):
                rope_sum(u, u + 3)
            batch(0, first=True)
            with pool.Fori(1, B - 1) as b:
                batch(b)
            batch(B - 1, last=True)
            skip(B - 1)

            pool.wait_ge(s_rows, 16 * (B + 1))
            pool.wait_ge(s_idx, 1)

            def gather(j, k, again=None):
                if again is not None:
                    pool.wait_ge(s_sca[k % 3], 16 * again)
                pool.tensor_copy(tok_now[:, k % 6:k % 6 + 1], slot_tok[:, bass.ds(j, 1)]).then_inc(s_now, 1)
                pool.wait_ge(s_now, j + 1)
                passed(pool)
                pool.indirect_dma_start(row_in[:, k % 6, :], None, tok_rows,
                                        bass.IndirectOffsetOnAxis(ap=tok_now[:, k % 6:k % 6 + 1], axis=0)
                                        ).then_inc(s_gat[k % 6], 16)

            def scatter(j, k):
                pool.wait_ge(s_comb, j + 1)
                passed(pool)
                pool.indirect_dma_start(out_v, bass.IndirectOffsetOnAxis(ap=tok_now[:, k % 6:k % 6 + 1], axis=0),
                                        row_out[:, k % 3, :], None, bounds_check=B * T - 1, oob_is_err=False
                                        ).then_inc(s_sca[k % 3], 16)

            for j in range(5):
                gather(j, j)
            for j in range(6):
                scatter(j, j)
                gather(j + 5, j + 5, None if j == 0 else (j - 1) // 3 + 1)
            with pool.Fori(1, NS // 6 - 1) as it:
                for k in range(6):
                    scatter(6 * it + k, k)
                    gather(6 * it + k + 5, k + 5, 2 * it + (k - 1) // 3 + 1)
            for j in range(NS // 6 * 6 - 6, NS):
                scatter(j, j)
                if j + 5 < NS:
                    gather(j + 5, j + 5, (j - 1) // 3 + 1)
            for k in range(3):
                pool.wait_ge(s_sca[k], 16 * (NS // 3))

        @block.scalar
        def _(act):
            act.wait_ge(s_const, 16)
            act.activation(ident_b[:, :], ident, ACT.Copy).then_inc(s_cb, 1)
            act.activation(mask_b[:, :], cst[:, C_MASK:C_MASK + P], ACT.Copy).then_inc(s_cb, 1)
            act.activation(lower_b[:, :], cst[:, C_LT:C_LT + P], ACT.Copy).then_inc(s_cb, 1)
            act.wait_ge(s_wraw, 48)
            for n in range(3):
                for c in range(KC):
                    act.activation(wh[:, n, c, :], w_raw[:, n, c, :], ACT.Copy).then_inc(s_whead, 1)

            def xt_head(n, g0):
                for c in range(KC):
                    act.wait_ge(s_ppdone, g0 + c + 1)
                    if not (isinstance(n, int) and n == 0):
                        pass
                    act.activation(xth[:, c, :], PP[c][:, :], ACT.Copy).then_inc(s_xth, 1)

            def v_out(g0, first):
                for m in range(2 * NI):
                    act.wait_ge(s_ppdone, g0 + m + 1 + (0 if first or m < 2 else NI))
                    act.activation(v[:, m // 2, (m % 2) * 512:(m % 2) * 512 + 512], PP[m % 2][:, :],
                                   ACT.Copy).then_inc(s_ppact, 1)

            def qk_out(b, u, tb):
                act.wait_ge(s_tbdone, tb + 1)
                i, kind, par = (u % 8) // 2, u % 2, (u // 8) % 2
                act.activation(qkt[:, par, kind, :, i * P:(i + 1) * P],
                               TB[:, :].rearrange("p (h t) -> p h t", h=G), ACT.Copy).then_inc(s_tbread, 1)

            def exps(b, h, i):
                n = 32 * b + 4 * h + i
                act.wait_ge(s_max, n + 1)
                act.activation(prob[:, h % 2, POFF[i]:POFF[i] + (i + 1) * P], SB[i % 2][:, 0:(i + 1) * P], ACT.Exp,
                               bias=negmax[:, h % 2, i:i + 1], scale=1.0,
                               accum_out=denom[:, h % 2, i:i + 1]).then_inc(s_exp, 1)

            def pt_out(b, h, c):
                act.wait_ge(s_ptdone, 24 * b + 3 * h + c + 1)
                lo = [0, 512, 896][c]
                w = 512 if c == 0 else 384
                act.activation(probt[:, h % 2, lo:lo + w], PT[(h + c) % 2][:, 0:w], ACT.Copy).then_inc(s_ptact, 1)

            def o_out(b, h):
                act.wait_ge(s_pv, 8 * b + h + 1)
                act.activation(ot[:, h, :], OB[:, :], ACT.Copy).then_inc(s_oread, 1)

            def xn_out(tb, c):
                act.wait_ge(s_tbdone, tb + 1)
                act.activation(xnt[:, c, :], TB[:, :], ACT.Copy).then_inc(s_tbread, 1)

            def aff_out(tb):
                act.wait_ge(s_tbdone, tb + 1)
                act.activation(aff[:, :, :], TB[:, 0:NI * E].rearrange("p (i e) -> p i e", i=NI),
                               ACT.Copy).then_inc(s_tbread, 1)

            def gate_exp(b):
                act.wait_ge(s_top, b + 1)
                act.activation(ealpha[:, :], top[:, :, 0], ACT.Exp, scale=-1.0).then_inc(s_ea, 1)

            def batch(b, first=False, last=False):
                tb = tbn(b, first)
                for h in range(H + 1):
                    if h < H:
                        unit = h < 4 or not last
                        exps(b, h, 0)
                        exps(b, h, 1)
                        if unit and h not in (0, 4):
                            qk_out(b, 2 * h + 7, tb)
                            tb = tb + 1
                        exps(b, h, 2)
                        exps(b, h, 3)
                    if h >= 1:
                        pt_out(b, h - 1, 0)
                    if h < H and unit:
                        qk_out(b, 2 * h + 8, tb)
                        tb = tb + 1
                    if h >= 1:
                        pt_out(b, h - 1, 2)
                        o_out(b, h - 1)
                    if h < H and not first and h == 2:
                        xn_out(tb, 0)
                        xn_out(tb + 1, 1)
                        tb = tb + 2
                    if h < H and not first and h == 3:
                        aff_out(tb)
                        tb = tb + 1
                    if h == 6 and not first:
                        gate_exp(b - 1)
                    if h == 3 or (h == 7 and not last):
                        qk_out(b, 2 * h + 9, tb)
                        tb = tb + 1
                    if h == 3 and not last:
                        xt_head(1, PPN(b) + 8)
                if not last:
                    v_out(PPN(b) + 18, False)

            xt_head(0, 0)
            for u in range(8):
                qk_out(0, u, u)
            v_out(10, True)
            batch(0, first=True)
            with act.Fori(1, B - 1) as b:
                batch(b)
            batch(B - 1, last=True)
            tb = tbn(B, False) - 8
            xn_out(tb, 0)
            xn_out(tb + 1, 1)
            aff_out(tb + 2)
            gate_exp(B - 1)

            def h1_out(j, k):
                act.wait_ge(s_h1, 2 * j + 1)
                act.activation(h1[:, k % 2, 0:512], FH[0][:, :], ACT.Copy).then_inc(s_h1a, 1)

            def h1t_out(j, k, e):
                act.wait_ge(s_hT, 2 * j + 1)
                for c in range(4):
                    ins = act.activation(h1t[:, k % 2, c, :], FT[0][:, c * P:(c + 1) * P], ACT.Relu,
                                         bias=b1_col[:, bass.ds(e, 1), c:c + 1].rearrange("p a b -> p (a b)"),
                                         scale=1.0)
                ins.then_inc(s_hTa, 1)

            act.wait_ge(s_texp, 1)
            act.wait_ge(s_fw, FW)

            def tile(j, k):
                e = act.value_load(tile_exp[0:1, bass.ds(j, 1)], min_val=0, max_val=E - 1)
                h1_out(j, k)
                h1t_out(j, k, e)

            with act.Fori(0, NS // 6) as it:
                for k in range(6):
                    tile(6 * it + k, k)
            for j in range(NS - 3, NS):
                tile(j, j)

        @block.tensor
        def _(pe):
            def mm3(out_ap, lh, ll, rh, rl, start, stop):
                pe.matmul(out_ap, ll, rh, start=start, stop=False)
                pe.matmul(out_ap, lh, rl, start=False, stop=False)
                return pe.matmul(out_ap, lh, rh, start=False, stop=stop)

            def xt(b_is_first, ready, dve):
                pe.wait_ge(s_xh, ready)
                for c in range(KC):
                    if not b_is_first:
                        pe.wait_ge(s_ppdve, dve - 1 + c)
                    for i in range(NI):
                        mm = pe.transpose(PP[c][:, i * P:(i + 1) * P], xh[:, i, c * P:(c + 1) * P], ident)
                    mm.then_inc(s_ppdone, 1)

            def unit_project(u, waits):
                g, i, kind = (u // 8) % 2, (u % 8) // 2, u % 2
                for s, n in waits:
                    pe.wait_ge(s, n)
                for c in range(KC):
                    mm = mm3(PP[u % 2][:, :], xth[:, c, i * P:(i + 1) * P], xtl[:, c, i * P:(i + 1) * P],
                             wh[:, kind, c, g * 512:g * 512 + 512], wl[:, kind, c, g * 512:g * 512 + 512],
                             c == 0, c == KC - 1)
                mm.then_inc(s_ppdone, 1)

            def unit_turn(n, u, tb):
                pe.wait_ge(s_rope, n + 1)
                pe.wait_ge(s_tbread, tb)
                for h in range(G):
                    mm = pe.transpose(TB[:, h * P:(h + 1) * P], rope[:, u % 2, h * P:(h + 1) * P], ident)
                mm.then_inc(s_tbdone, 1)

            def v_project(m, waits):
                for s, n in waits:
                    pe.wait_ge(s, n)
                i, half = m // 2, m % 2
                for c in range(KC):
                    mm = mm3(PP[m % 2][:, :], xth[:, c, i * P:(i + 1) * P], xtl[:, c, i * P:(i + 1) * P],
                             wh[:, 2, c, half * 512:half * 512 + 512], wl[:, 2, c, half * 512:half * 512 + 512],
                             c == 0, c == KC - 1)
                mm.then_inc(s_ppdone, 1)

            def score(b, h, i, tb_need):
                if tb_need is not None:
                    pe.wait_ge(s_tbread, tb_need)
                n = 32 * b + 4 * h + i
                if not (isinstance(b, int) and n < 2):
                    pe.wait_ge(s_exp, n - 1)
                w = (i + 1) * P
                par, hh = h // G, h % G
                pe.matmul(SB[i % 2][:, 0:w], qkt[:, par, 0, hh, i * P:(i + 1) * P], qkt[:, par, 1, hh, 0:w],
                          start=True, stop=False)
                pe.matmul(SB[i % 2][:, i * P:w], ident_b[:, :], mask_b[:, :],
                          start=False, stop=True).then_inc(s_score, 1)

            def turn_probs(b, h, c):
                if c == 0:
                    pe.wait_ge(s_pscaled, 8 * b + h + 1)
                n_act, n_dve = 16 * b + 2 * h, 8 * b + h
                zero = isinstance(b, int) and b == 0 and h == 0
                if not zero:
                    if c == 0:
                        pe.wait_ge(s_ptdve, n_dve)
                    if c == 1:
                        pe.wait_ge(s_ptact, n_act)
                if c == 2:
                    pe.wait_ge(s_ptact, n_act + 1)
                dst = PT[(h + c) % 2]
                for j in ((0,), (1,), (2, 3))[c]:
                    for i in range(j, NI):
                        o = TOFF[j] - [0, 512, 896][c] + (i - j) * P
                        mm = pe.transpose(dst[:, o:o + P], prob[:, h % 2, POFF[i] + j * P:POFF[i] + (j + 1) * P],
                                          ident)
                mm.then_inc(s_ptdone, 1)

            def attend(b, h, need_v):
                if need_v is not None:
                    pe.wait_ge(s_ppact, need_v)
                if not (isinstance(b, int) and b == 0 and h == 0):
                    pe.wait_ge(s_oread, 8 * b + h)
                pe.wait_ge(s_ptact, 16 * b + 2 * h + 1)
                for j in range(NI):
                    if j == 1:
                        pe.wait_ge(s_ptdve, 8 * b + h + 1)
                    if j == 2:
                        pe.wait_ge(s_ptact, 16 * b + 2 * h + 2)
                    mm = pe.matmul(OB[:, j * P:T], v[:, j, h * P:(h + 1) * P],
                                   probt[:, h % 2, TOFF[j]:TOFF[j] + (NI - j) * P],
                                   start=(j == 0), stop=(j == NI - 1))
                mm.then_inc(s_pv, 1)

            def out_project(b, i, waits):
                pe.wait_ge(s_oread, 8 * b + 8)
                for s, n in waits:
                    pe.wait_ge(s, n)
                for h in range(H):
                    mm = pe.matmul(PP[i % 2][:, 0:D], ot[:, h, i * P:(i + 1) * P], wo[:, h, :],
                                   start=(h == 0), stop=(h == H - 1))
                mm.then_inc(s_ppdone, 1)

            def xn_turn(b, tb, c):
                if c == 0:
                    pe.wait_ge(s_xn, b + 1)
                pe.wait_ge(s_tbread, tb)
                for i in range(NI):
                    mm = pe.transpose(TB[:, i * P:(i + 1) * P], xn[:, i, c * P:(c + 1) * P], ident)
                mm.then_inc(s_tbdone, 1)

            def affinity(tb):
                pe.wait_ge(s_tbread, tb)
                for i in range(NI):
                    for c in range(KC):
                        mm = pe.matmul(TB[:, i * E:(i + 1) * E], xnt[:, c, i * P:(i + 1) * P], cent[:, c, :],
                                       start=(c == 0), stop=(c == KC - 1))
                mm.then_inc(s_tbdone, 1)

            def batch(b, first=False, last=False):
                tb = tbn(b, first)
                dve, actn = DVE0(b), ACT0(b)
                for h in range(H + 1):
                    unit = h < 4 or (h < H and not last)
                    if h < H:
                        score(b, h, 0, tb if h in (0, 4) else None)
                        score(b, h, 1, None)
                    if unit:
                        u = 2 * h + 8
                        pos0 = dve + 2 * h + (0 if h < 4 else 2)
                        if h == 0:
                            unit_project(u, [(s_ppact, actn - 1)])
                        elif h == 4:
                            unit_project(u, [(s_ppdve, pos0)])
                        else:
                            unit_project(u, [(s_ppdve, pos0 - 1)])
                        if h not in (0, 4):
                            unit_turn(UN(b) - 8 + u - 1, u - 1, tb)
                            tb = tb + 1
                    if h < H:
                        score(b, h, 2, None)
                        score(b, h, 3, None)
                    if unit:
                        u = 2 * h + 9
                        if h == 0:
                            unit_project(u, [(s_ppact, actn)])
                        else:
                            unit_project(u, [(s_ppdve, pos0)])
                    if h >= 1:
                        turn_probs(b, h - 1, 0)
                        turn_probs(b, h - 1, 1)
                    if unit:
                        unit_turn(UN(b) - 8 + u - 1, u - 1, tb)
                        tb = tb + 1
                    if h >= 1:
                        turn_probs(b, h - 1, 2)
                        attend(b, h - 1, actn if h == 1 else None)
                    if not first and h == 2:
                        xn_turn(b - 1, tb, 0)
                        xn_turn(b - 1, tb + 1, 1)
                        tb = tb + 2
                    if not first and h == 3:
                        affinity(tb)
                        tb = tb + 1
                    if h == 3 or (h == 7 and not last):
                        unit_turn(UN(b) - 8 + 2 * h + 9, 2 * h + 9, tb)
                        tb = tb + 1
                    if h == 3 and not last:
                        xt(False, b + 2, dve + 8)
                r0 = dve + (18 if not last else 8)
                if not last:
                    v_project(0, [(s_ppdve, r0 - 1)])
                    v_project(1, [(s_ppdve, r0)])
                for i in range(NI):
                    out_project(b, i, [(s_ppdve, r0 - 1 + i)] if last or i >= 2 else [(s_ppact, actn + i + 1)])
                if not last:
                    for m in range(2, 2 * NI):
                        v_project(m, [(s_ppdve, r0 + 1 + m)] if m < 4 else [(s_ppact, actn + m - 1)])

            pe.wait_ge(s_const, 16)
            xt(True, 1, 0)
            pe.wait_ge(s_wrest, 6)
            for u in range(8):
                if u < 1:
                    unit_project(u, [(s_ppdve, 2)])
                else:
                    unit_project(u, [(s_ppdve, u + 1)])
                if u >= 1:
                    unit_turn(u - 1, u - 1, u - 1)
            for m in range(2 * NI):
                v_project(m, [(s_ppdve, 9 + m)] if m < 2 else [(s_ppact, m - 1)])
                if m == 0:
                    unit_turn(7, 7, 7)
            pe.wait_ge(s_cb, 5)
            pe.wait_ge(s_wsmall, 32)
            batch(0, first=True)
            with pe.Fori(1, B - 1) as b:
                batch(b)
            batch(B - 1, last=True)
            tb = tbn(B, False) - 8
            xn_turn(B - 1, tb, 0)
            xn_turn(B - 1, tb + 1, 1)
            affinity(tb + 2)

            pe.wait_ge(s_hot, B)
            oh = onehot[:, :, :].rearrange("p t e -> p (t e)")
            pe.matmul(SB[0][:, 0:NT * E], lower_b[:, :], oh, start=True, stop=True)
            pe.matmul(SB[1][:, 0:NT * E], ones_b[:, :], oh, start=True, stop=True).then_inc(s_count, 1)
            for t in range(NT):
                if t % 4 == 0:
                    pe.wait_ge(s_route, t // 4 + 1)
                mm = pe.matmul(PT[0][:, 0:NS], hot_lo[:, t % 8, :], hot_hi[:, t % 8, :],
                               start=(t == 0), stop=(t == NT - 1))
                if t % 4 == 3:
                    mm.then_inc(s_routeb, 1)

            def turn_z(j, k, used):
                pe.wait_ge(s_gat[k % 6], 16 * used + 16)
                if not (isinstance(j, int) and j == 0):
                    pe.wait_ge(s_ht, j)
                for c in range(KC):
                    mm = pe.transpose(FZ[:, c * P:(c + 1) * P], row_in[:, k % 6, c * P:(c + 1) * P], ident)
                mm.then_inc(s_zt, 1)

            def up(j, k, e):
                pe.wait_ge(s_ht, j + 1)
                if not (isinstance(j, int) and j == 0):
                    pe.wait_ge(s_h1a, j)
                for half in range(2):
                    if half == 1 and not (isinstance(j, int) and j == 0):
                        pe.wait_ge(s_h1d, j)
                    for c in range(KC):
                        mm = pe.matmul(FH[half][:, :], ht[:, k % 2, c, :],
                                       w12[:, bass.ds(e, 1), c * F + half * 512:c * F + half * 512 + 512
                                           ].rearrange("p o f -> p (o f)"),
                                       start=(c == 0), stop=(c == KC - 1))
                    mm.then_inc(s_h1, 1)

            def turn_h(j, k):
                for half in range(2):
                    if half == 0:
                        pe.wait_ge(s_h1a, j + 1)
                    else:
                        pe.wait_ge(s_h1d, j + 1)
                    if not (isinstance(j, int) and j == 0):
                        pe.wait_ge(s_hTa if half == 0 else s_hTd, j)
                    for c in range(4):
                        mm = pe.transpose(FT[half][:, c * P:(c + 1) * P],
                                          h1[:, k % 2, half * 512 + c * P:half * 512 + (c + 1) * P], ident)
                    mm.then_inc(s_hT, 1)

            def down(j, k, e):
                if not (isinstance(j, int) and j == 0):
                    pe.wait_ge(s_yb, j)
                for c in range(FC):
                    if c == 0:
                        pe.wait_ge(s_hTa, j + 1)
                    if c == 4:
                        pe.wait_ge(s_hTd, j + 1)
                    mm = pe.matmul(FY[k % 2][:, 0:D], h1t[:, k % 2, c, :],
                                   w12[:, bass.ds(e, 1), KC * F + c * D:KC * F + (c + 1) * D
                                       ].rearrange("p o d -> p (o d)"),
                                   start=(c == 0), stop=(c == FC - 1))
                mm.then_inc(s_y, 1)

            pe.wait_ge(s_texp, 1)
            pe.wait_ge(s_fw, FW)

            def expert(j):
                return pe.value_load(tile_exp[0:1, bass.ds(j, 1)], min_val=0, max_val=E - 1)

            e0 = expert(0)
            turn_z(0, 0, 0)
            up(0, 0, e0)
            e1 = expert(1)
            turn_h(0, 0)
            turn_z(1, 1, 0)

            def step(j, k, used, e_j, e_next):
                up(j + 1, k + 1, e_next)
                turn_z(j + 2, k + 2, used)
                down(j, k, e_j)
                e_after = expert(j + 2)
                turn_h(j + 1, k + 1)
                return e_next, e_after

            for j in range(3):
                e0, e1 = step(j, j, (j + 2) // 6, e0, e1)
            with pe.Fori(0, NS // 6 - 1) as it:
                ea, eb = expert(6 * it + 3), expert(6 * it + 4)
                for k in range(6):
                    ea, eb = step(6 * it + 3 + k, 3 + k, it + (k + 5) // 6, ea, eb)
            e0, e1 = expert(NS - 6), expert(NS - 5)
            for j in range(NS - 6, NS - 2):
                e0, e1 = step(j, j, (j + 2) // 6, e0, e1)
            up(NS - 1, NS - 1, e1)
            down(NS - 2, NS - 2, e0)
            turn_h(NS - 1, NS - 1)
            down(NS - 1, NS - 1, e1)

        @block.vector
        def _(dve):
            def norm_stats(k, src, made):
                for i in range(NI):
                    ins = dve.bn_stats(stats[k][:, i, :], src[:, i, :])
                ins.then_inc(made, 1)

            def norm_aggr(k, own, n, made):
                dve.wait_ge(own, n)
                passed(dve)
                for i in range(NI):
                    ins = dve.bn_aggr(mv[k][:, i, :], stats[k][:, i, :])
                ins.then_inc(made, 1)

            def norm_apply(k, dst, src, rdy, n, made):
                dve.wait_ge(rdy, n)
                for i in range(NI):
                    ins = dve.tensor_scalar(dst[:, i, 0:D], src[:, i, :], mv[k][:, i, 0:1], rstd[k][:, i:i + 1],
                                            ALU.subtract, ALU.mult)
                ins.then_inc(made, 1)

            def ln_x_stats(b):
                dve.wait_ge(s_xa, 16 * (b + 1))
                norm_stats(0, xa, s_lnx)
                norm_aggr(0, s_lnx, b + 1, s_xmean)

            def ln_x(b, g0):
                if g0 is not None:
                    dve.wait_ge(s_ppdone, g0)
                norm_apply(0, xh, xa, s_xrstd, b + 1, s_xh)

            def xt_rest(n, g0):
                for c in range(KC):
                    dve.wait_ge(s_xth, n + c + 1)
                    dve.tensor_tensor(xtl[:, c, :], PP[c][:, :], xth[:, c, :].bitcast(F32),
                                      ALU.subtract).then_inc(s_ppdve, 1)

            def rotate(n, u, g, free):
                i, kind = (u % 8) // 2, u % 2
                cc, ss = (C_COSQ, C_SINQ) if kind == 0 else (C_COSK, C_SINK)
                cos = cst[:, cc + i * 64:cc + (i + 1) * 64].rearrange("p (o d) -> p o d", o=1)
                sin = cst[:, ss + i * P:ss + (i + 1) * P].rearrange("p (o s d) -> p o s d", o=1, s=2)
                dve.wait_ge(s_ppdone, g)
                if free is not None:
                    dve.wait_ge(s_rope, n - 1)
                    dve.wait_ge(s_tbdone, free)
                src = PP[u % 2][:, :].rearrange("p (h s d) -> p h s d", h=G, s=2)
                dc = rope_c[:, u % 2, :].rearrange("p (h s d) -> p h s d", h=G, s=2)
                ds_ = rope_s[:, u % 2, :].rearrange("p (h s d) -> p h s d", h=G, s=2)
                dve.tensor_tensor(rope_c[:, u % 2, :].rearrange("p (a d) -> p a d", d=64),
                                  PP[u % 2][:, :].rearrange("p (a d) -> p a d", d=64),
                                  cos.broadcast_to([P, 2 * G, 64]), ALU.mult)
                dve.tensor_tensor(ds_[:, :, 0, :], src[:, :, 1, :], sin[:, :, 0, :].broadcast_to([P, G, 64]),
                                  ALU.mult)
                ins = dve.tensor_tensor(ds_[:, :, 1, :], src[:, :, 0, :], sin[:, :, 1, :].broadcast_to([P, G, 64]),
                                        ALU.mult)
                ins.then_inc(s_ppdve, 1)

            def row_max(b, h, i):
                n = 32 * b + 4 * h + i
                dve.wait_ge(s_score, n + 1)
                dve.tensor_reduce(negmax[:, h % 2, i:i + 1], SB[i % 2][:, 0:(i + 1) * P], AX.X, ALU.max,
                                  negate=True).then_inc(s_max, 1)

            def recip(b, h):
                dve.wait_ge(s_exp, 32 * b + 4 * h + 4)
                dve.reciprocal(rdenom[:, h % 2, :], denom[:, h % 2, :]).then_inc(s_rden, 1)
                dve.wait_ge(s_rden, 8 * b + h + 1)
                for i in range(NI):
                    p_i = prob[:, h % 2, POFF[i]:POFF[i] + (i + 1) * P]
                    ins = dve.tensor_scalar(p_i, p_i, rdenom[:, h % 2, i:i + 1], None, ALU.mult)
                ins.then_inc(s_pscaled, 1)

            def pt_out(b, h):
                dve.wait_ge(s_ptdone, 24 * b + 3 * h + 2)
                dve.tensor_copy(probt[:, h % 2, 512:896], PT[(h + 1) % 2][:, 0:384]).then_inc(s_ptdve, 1)

            def residual(b, i, g):
                if i == 0:
                    dve.wait_ge(s_xr, 16 * (b + 1))
                dve.wait_ge(s_ppdone, g)
                dve.tensor_tensor(x1[:, i, :], PP[i % 2][:, 0:D], xr[:, i, :], ALU.add).then_inc(s_ppdve, 1)

            def choose(b):
                passed(dve)
                for i in range(NI):
                    ins = dve.max(top[:, i, :], aff[:, i, :])
                ins.then_inc(s_top, 1)
                dve.wait_ge(s_top, b + 1)
                passed(dve)
                for i in range(NI):
                    ins = dve.max_index(topi[:, i, :], top[:, i, :], aff[:, i, :])
                ins.then_inc(s_topi, 1)
                dve.wait_ge(s_topi, b + 1)
                dve.tensor_copy(topf[:, :], topi[:, :, 0]).then_inc(s_topf, 1)
                dve.wait_ge(s_topf, b + 1)
                dve.tensor_tensor(onehot[:, bass.ds(NI * b, NI), :],
                                  cst[:, C_IOTA:C_IOTA + E].rearrange("p (o e) -> p o e", o=1).broadcast_to([P, NI, E]),
                                  topf[:, :].rearrange("p (i o) -> p i o", o=1).broadcast_to([P, NI, E]),
                                  ALU.is_equal).then_inc(s_hot, 1)

            def gate(b):
                dve.wait_ge(s_ea, b + 1)
                dve.tensor_scalar(ealpha1[:, :], ealpha[:, :], 1.0, None, ALU.add).then_inc(s_ea1, 1)
                dve.wait_ge(s_ea1, b + 1)
                dve.reciprocal(rows[:, :, 2 * D], ealpha1[:, :]).then_inc(s_gate, 1)

            def batch(b, first=False, last=False):
                g, un = PPN(b), UN(b) - 8
                tb = tbn(b, first)
                tb_at = {}
                for h in range(H + 1):
                    unit = h < 4 or (h < H and not last)
                    if h < H:
                        row_max(b, h, 0)
                        row_max(b, h, 1)
                    if unit:
                        u = 2 * h + 8
                        gu = g + 2 * h + 1 + (0 if h < 4 else 2)
                        rotate(un + u, u, gu, tb_of(b, first, u - 2))
                    if h < H:
                        row_max(b, h, 2)
                        row_max(b, h, 3)
                    if unit:
                        u = 2 * h + 9
                        rotate(un + u, u, gu + 1, tb_of(b, first, u - 2))
                    if h >= 1:
                        pt_out(b, h - 1)
                    if h < H:
                        recip(b, h)
                    if h == 0 and not last:
                        ln_x_stats(b + 1)
                    if h == 1 and not last:
                        ln_x(b + 1, g - 20 if not first else 2)
                    if not first and h == 1:
                        dve.wait_ge(s_rows, 16 * b)
                        norm_apply(2, rows, xn, s_zrstd, b, s_z)
                    if not first and h == 4:
                        dve.wait_ge(s_tbread, tb + 10)
                        choose(b - 1)
                    if not first and h == 7:
                        gate(b - 1)
                    if h == 3 and not last:
                        xt_rest(2 * (b + 1), None)
                r0 = g + (20 if not last else 8)
                for i in range(NI):
                    residual(b, i, r0 + i + 1)
                dve.wait_ge(s_ppdve, DVE0(b) + (22 if not last else 12))
                norm_stats(1, x1, s_lnn)
                norm_aggr(1, s_lnn, b + 1, s_nstat)
                if not first:
                    dve.wait_ge(s_skip, b)
                norm_apply(1, xn, x1, s_nrstd, b + 1, s_xn)
                dve.wait_ge(s_xn, b + 1)
                norm_stats(2, xn, s_lnz)
                norm_aggr(2, s_lnz, b + 1, s_zstat)

            def tb_of(b, first, u):
                t = tbn(b, first)
                if u < 8:
                    return t - (7 - u) if u >= 6 else None
                n = u - 8 + 1
                if u >= 15 and not first:
                    n += 3
                elif u >= 13 and not first:
                    n += 2 if u >= 13 else 0
                return t + n

            s_lnx, s_lnn, s_lnz, s_topi, s_topf, s_ea1 = s_own

            dve.wait_ge(s_const, 16)
            ln_x_stats(0)
            ln_x(0, None)
            for n in range(3):
                for c in range(KC):
                    dve.wait_ge(s_whead, 2 * n + c + 1)
                    dve.tensor_tensor(wl[:, n, c, :], w_raw[:, n, c, :], wh[:, n, c, :].bitcast(F32),
                                      ALU.subtract).then_inc(s_wrest, 1)
            xt_rest(0, 0)
            for u in range(8):
                rotate(u, u, 3 + u, (u - 1) if u >= 2 else None)
            batch(0, first=True)
            with dve.Fori(1, B - 1) as b:
                batch(b)
            batch(B - 1, last=True)
            dve.wait_ge(s_rows, 16 * B)
            norm_apply(2, rows, xn, s_zrstd, B, s_z)
            dve.wait_ge(s_tbread, tbn(B, False) - 8 + 3)
            choose(B - 1)
            gate(B - 1)

            rc = [0]

            def own(ins):
                rc[0] += 1
                ins.then_inc(s_dve, 1)
                dve.wait_ge(s_dve, rc[0])

            flat = lambda a: a[:, :, :].rearrange("p a b -> p (a b)")
            dve.wait_ge(s_count, 1)
            own(dve.tensor_copy(tot[:, :, :].rearrange("p e t -> p t e"),
                                SB[1][:, 0:NT * E].rearrange("p (t e) -> p t e", e=E)))
            own(dve.tensor_tensor_scan(flat(cum), ones_f[:, :], flat(tot), 0.0, ALU.mult, ALU.add))
            own(dve.tensor_copy(cnt[:, :], cum[:, :, NT - 1]))
            own(dve.tensor_tensor(adj2[:, 1:E], cnt[:, 1:E], cnt[:, 0:E - 1], ALU.subtract))
            own(dve.tensor_copy(adj2[:, 0:1], cnt[:, 0:1]))
            own(dve.tensor_scalar(cnt_i[:, :], adj2[:, :], float(P - 1), None, ALU.add))
            own(dve.tensor_scalar(tiles_i[:, :], cnt_i[:, :], 7, None, ALU.logical_shift_right))
            own(dve.tensor_copy(tiles_f[:, :], tiles_i[:, :]))
            own(dve.tensor_tensor_scan(tiles_cum[:, :], ones_f[:, 0:E], tiles_f[:, :], 0.0, ALU.mult, ALU.add))
            own(dve.tensor_tensor(adj[:, :], tiles_cum[:, :], tiles_f[:, :], ALU.subtract))
            own(dve.scalar_tensor_tensor(adj[:, :], adj[:, :], float(P), cnt[:, :], ALU.mult, ALU.subtract))
            own(dve.tensor_tensor(adj[:, :], adj[:, :], adj2[:, :], ALU.add))
            own(dve.tensor_tensor(flat(cum), flat(cum), flat(tot), ALU.subtract))
            own(dve.tensor_tensor(cum[:, :, :], cum[:, :, :],
                                  adj[:, :].rearrange("p (e o) -> p e o", o=1).broadcast_to([P, E, NT]), ALU.add))
            own(dve.tensor_tensor(pos[:, :, :], SB[0][:, 0:NT * E].rearrange("p (t e) -> p t e", e=E),
                                  cum[:, :, :].rearrange("p e t -> p t e"), ALU.add))
            own(dve.tensor_tensor(pos[:, :, :], pos[:, :, :], onehot[:, :, :], ALU.mult))
            own(dve.tensor_reduce(slot[:, :], pos[:, :, :], AX.X, ALU.add))
            own(dve.tensor_copy(slot_i[:, :], slot[:, :]))
            own(dve.tensor_scalar(hi_i[:, :], slot_i[:, :], 7, None, ALU.logical_shift_right))
            own(dve.tensor_scalar(lo_i[:, :], slot_i[:, :], P - 1, None, ALU.bitwise_and))
            own(dve.tensor_copy(slot_hi[:, :], hi_i[:, :]))
            own(dve.tensor_copy(slot_lo[:, :], lo_i[:, :]))
            wide = lambda a, n: a.rearrange("p (t o) -> p t o", o=1).broadcast_to([P, 4, n])
            count = lambda n: cst[:, C_IOTA:C_IOTA + n].rearrange("p (o n) -> p o n", o=1).broadcast_to([P, 4, n])
            for g in range(NT // 4):
                ts, k = slice(4 * g, 4 * g + 4), slice(g % 2 * 4, g % 2 * 4 + 4)
                if g >= 2:
                    dve.wait_ge(s_routeb, g - 1)
                dve.tensor_tensor(hot_hi[:, k, :], count(NS), wide(slot_hi[:, ts], NS),
                                  ALU.is_equal).then_inc(s_hhi, 1)
                dve.tensor_tensor(hot_lo[:, k, :], count(P), wide(slot_lo[:, ts], P), ALU.is_equal)
                dve.wait_ge(s_hhi, g + 1)
                dve.tensor_tensor(hot_hi[:, k, :], hot_hi[:, k, :],
                                  wide(cst[:, C_TOK + 4 * g:C_TOK + 4 * g + 4], NS), ALU.mult).then_inc(s_route, 1)
            own(dve.tensor_tensor(below[:, :, :],
                                  tiles_cum[:, :].rearrange("p (o e) -> p o e", o=1).broadcast_to([P, NS, E]),
                                  cst[:, C_IOTA:C_IOTA + NS].rearrange("p (j o) -> p j o", o=1).broadcast_to([P, NS, E]),
                                  ALU.is_le))
            own(dve.tensor_reduce(below_n[:, :], below[:, :, :], AX.X, ALU.add))
            dve.tensor_scalar(tile_exp[:, :], below_n[:, :], float(E - 1), None, ALU.min).then_inc(s_texp, 1)
            dve.wait_ge(s_routeb, NT // 4)
            dve.tensor_scalar(slot_tok[:, :], PT[0][:, 0:NS], float(B * T), None, ALU.add).then_inc(s_idx, 1)

            dve.wait_ge(s_texp, 1)
            dve.wait_ge(s_fw, FW)

            def affine(j, k, e):
                dve.wait_ge(s_zt, j + 1)
                for c in range(KC):
                    ins = dve.tensor_scalar(ht[:, k % 2, c, :], FZ[:, c * P:(c + 1) * P],
                                            g_col[:, bass.ds(e, 1), c:c + 1].rearrange("p a b -> p (a b)"),
                                            b_col[:, bass.ds(e, 1), c:c + 1].rearrange("p a b -> p (a b)"),
                                            ALU.mult, ALU.add)
                ins.then_inc(s_ht, 1)

            def h1_out(j, k):
                dve.wait_ge(s_h1, 2 * j + 2)
                dve.tensor_copy(h1[:, k % 2, 512:1024], FH[1][:, :]).then_inc(s_h1d, 1)

            def h1t_out(j, k, e):
                dve.wait_ge(s_hT, 2 * j + 2)
                for c in range(4, 8):
                    ins = dve.tensor_scalar(h1t[:, k % 2, c, :], FT[1][:, (c - 4) * P:(c - 3) * P],
                                            b1_col[:, bass.ds(e, 1), c:c + 1].rearrange("p a b -> p (a b)"), 0.0,
                                            ALU.add, ALU.max)
                ins.then_inc(s_hTd, 1)

            def combine(j, k, e, again):
                dve.wait_ge(s_y, j + 1)
                dve.tensor_tensor(yb[:, k % 2, :], FY[k % 2][:, 0:D],
                                  b2_all[:, bass.ds(e, 1), :].rearrange("p o d -> p (o d)"),
                                  ALU.add).then_inc(s_yb, 1)
                if again is not None:
                    dve.wait_ge(s_sca[k % 3], 16 * again)
                dve.wait_ge(s_yb, j + 1)
                dve.scalar_tensor_tensor(row_out[:, k % 3, :], yb[:, k % 2, :], row_in[:, k % 6, 2 * D:2 * D + 1],
                                         row_in[:, k % 6, D:2 * D], ALU.mult, ALU.add).then_inc(s_comb, 1)

            def expert(j):
                return dve.value_load(tile_exp[0:1, bass.ds(j, 1)], min_val=0, max_val=E - 1)

            e = expert(0)
            affine(0, 0, e)
            h1_out(0, 0)
            h1t_out(0, 0, e)
            affine(1, 1, expert(1))

            def step(j, k, again, left=3):
                if left > 2:
                    e2 = expert(j + 2)
                if left > 1:
                    h1_out(j + 1, k + 1)
                if left > 2:
                    affine(j + 2, k + 2, e2)
                combine(j, k, expert(j), again)
                if left > 1:
                    h1t_out(j + 1, k + 1, expert(j + 1))

            for j in range(3):
                step(j, j, None)
            with dve.Fori(0, NS // 6 - 1) as it:
                for k in range(6):
                    step(6 * it + 3 + k, 3 + k, 2 * it + 1 + k // 3)
            for j in range(NS - 6, NS):
                step(j, j, j // 3, NS - j)


_INS = ["x", "w_q", "w_k", "w_v", "w_o", "cent_t", "ln_g", "ln_b", "w1_t", "b1", "w2_t", "b2", "consts"]


def constants():
    import numpy as np
    f = np.float32
    c = np.zeros((P, C_END), f)
    half = DH // 2
    freqs = np.power(f(10000.0), -(np.arange(half, dtype=f) / f(half))).astype(f)
    rad = (np.arange(T, dtype=f)[:, None] * freqs[None, :]).astype(f)
    cos, sin = np.cos(rad).astype(f), np.sin(rad).astype(f)
    for c_cos, c_sin, s in ((C_COSQ, C_SINQ, f(1.0 / DH)), (C_COSK, C_SINK, f(1.0))):
        for i in range(NI):
            t = slice(i * P, (i + 1) * P)
            c[:, c_cos + i * 64:c_cos + (i + 1) * 64] = cos[t] * s
            c[:, c_sin + i * P:c_sin + i * P + 64] = -sin[t] * s
            c[:, c_sin + i * P + 64:c_sin + (i + 1) * P] = sin[t] * s
    c[:, C_IOTA:C_IOTA + P] = np.arange(P)[None, :]
    c[:, C_TOK:C_TOK + NT] = np.arange(P)[:, None] + P * np.arange(NT)[None, :] - B * T
    c[:, C_ID:C_ID + P] = np.eye(P)
    p, n = np.arange(P)[:, None], np.arange(P)[None, :]
    c[:, C_MASK:C_MASK + P] = np.where(n > p, f(-1e30), f(0.0))
    c[:, C_LT:C_LT + P] = (p < n)
    return c


def kernel(**inputs):
    import numpy as np
    import concourse.bacc as bacc
    from concourse.bass_utils import run_bass_kernel_spmd

    g = {k[3:]: np.asarray(a) for k, a in inputs.items()}
    arrays = {
        "x": g["attn_x"], "w_q": g["attn_w_aq"].reshape(D, H * DH), "w_k": g["attn_w_ak"].reshape(D, H * DH),
        "w_v": g["attn_w_av"].reshape(D, H * DH), "w_o": g["attn_w_ao"].reshape(H * DH, D),
        "cent_t": g["ffn_centroids"].T, "ln_g": g["ffn_ln_g"], "ln_b": g["ffn_ln_b"],
        "w1_t": g["ffn_w1"].transpose(0, 2, 1), "b1": g["ffn_b1"],
        "w2_t": g["ffn_w2"].transpose(0, 2, 1), "b2": g["ffn_b2"], "consts": constants(),
    }
    arrays = {k: np.ascontiguousarray(a) for k, a in arrays.items()}
    nc = bacc.Bacc("TRN2", target_bir_lowering=False, num_devices=1)
    ins = [nc.dram_tensor(k, arrays[k].shape, F32, kind="ExternalInput").ap() for k in _INS]
    out = nc.dram_tensor("out", (B, T, D), F32, kind="ExternalOutput").ap()
    tok_rows = nc.dram_tensor("tok_rows", (B * T + 1, ROW), F32, kind="Internal").ap()
    build(nc, *ins, out, tok_rows)
    r = run_bass_kernel_spmd(nc, [arrays], core_ids=[0])
    return r.results[0]["out"]
```

```python
from contextlib import ExitStack

import concourse.bass as bass
from concourse import mybir

F32 = mybir.dt.float32
F32R = mybir.dt.float32r
BF16 = mybir.dt.bfloat16
I32 = mybir.dt.int32
U32 = mybir.dt.uint32
ACT = mybir.ActivationFunctionType
ALU = mybir.AluOpType
AX = mybir.AxisListType

P = 128
EPS = 1e-5
B, T, D = 8, 512, 256
H, DH = 8, 128
E, F = 8, 1024
NI = T // P
KC = D // P
FC = F // P
NT = B * NI
NS = NT + E - 1
ROW = 2 * D + 4
POFF = [0, 128, 384, 768]
TOFF = [0, 512, 896, 1152]
CAUSAL = NI * (NI + 1) // 2 * P
CHUNK = [(0, 512), (512, 384), (896, 384)]

C_COS, C_SIN = 0, T
C_IOTA = 2 * T
C_TOK = C_IOTA + P
C_ID = C_TOK + NT
C_MASK = C_ID + P
C_LT = C_MASK + P
C_END = C_LT + P


def build(nc, x, w_q, w_k, w_v, w_o, cent_t, ln_g, ln_b, w1_t, b1, w2_t, b2, consts, out, tok_rows):
    ctx = ExitStack()
    with ctx:
        sem = lambda n: ctx.enter_context(nc.semaphore(n))

        base = (nc.sbuf_base + 63) // 64 * 64
        place = [base]
        size = {F32: 4, F32R: 4, BF16: 2, I32: 4, U32: 4}

        def sb(name, shape, dt):
            n = size[dt]
            for s in shape[1:]:
                n *= s
            t = nc.alloc_sbuf_tensor_at(name, shape, dt, offset=place[0])
            place[0] += (n + 31) // 32 * 32
            assert place[0] <= nc.sbuf_usable_end, (name, place[0])
            return t

        onehot = sb("onehot", [P, NT, E], BF16)
        cst = sb("cst", [P, C_END], F32)
        ident = cst[:, C_ID:C_ID + P]
        ident_b = sb("ident_b", [P, P], BF16)
        mask_b = sb("mask_b", [P, P], BF16)
        lower_b = sb("lower_b", [P, P], BF16)
        ones_b = sb("ones_b", [P, P], BF16)
        cent = sb("cent", [P, KC, E], F32)
        slot_hi = sb("slot_hi", [P, NT], F32)
        slot_lo = sb("slot_lo", [P, NT], F32)
        slot_tok = sb("slot_tok", [P, NS], U32)
        tok_now = sb("tok_now", [P, 6], U32)
        tile_exp = sb("tile_exp", [P, NS], I32)
        ones_f = sb("ones_f", [P, E * NT], F32)
        common_end = place[0]

        xa = sb("xa", [P, NI, D], F32)
        xh = sb("xh", [P, NI, D], F32)
        xth = sb("xth", [P, KC, T], F32R)
        xtl = sb("xtl", [P, KC, T], F32R)
        wh = sb("wh", [P, 3, KC, H * DH], F32R)
        wl = sb("wl", [P, 3, KC, H * DH], F32R)
        w_raw_at = place[0]
        qkh = sb("qkh", [P, 4, 2, T], F32R)
        qkl = sb("qkl", [P, 4, 2, T], F32R)
        rope_c = sb("rope_c", [P, 2, T], F32)
        rope_s = sb("rope_s", [P, 2, T], F32)
        w_raw = nc.alloc_sbuf_tensor_at("w_raw", [P, 3, KC, H * DH], F32, offset=w_raw_at)
        prob = sb("prob", [P, 2, CAUSAL], F32)
        wo = sb("wo", [P, H, D], F32)
        vh = sb("vh", [P, NI, H * DH], F32R)
        vl = sb("vl", [P, NI, H * DH], F32R)
        xr = sb("xr", [P, NI, D], F32)
        routing_at = place[0]
        pth = sb("pth", [P, CAUSAL], F32R)
        ptl = sb("ptl", [P, CAUSAL], F32R)
        ot = sb("ot", [P, H, T], F32)
        routing_end = place[0]
        x1 = sb("x1", [P, NI, D], F32)
        xn = sb("xn", [P, NI, D], F32)
        xnt = sb("xnt", [P, KC, T], F32)
        gates = sb("gates", [P, NI, ROW - 2 * D], F32)
        negmax = sb("negmax", [P, 2, NI], F32)
        denom = sb("denom", [P, 2, NI], F32)
        rdenom = sb("rdenom", [P, 2, NI], F32)
        stats = [sb(f"stats{k}", [P, NI, 6], F32) for k in range(3)]
        mv = [sb(f"mv{k}", [P, NI, 2], F32) for k in range(3)]
        veps = [sb(f"veps{k}", [P, NI], F32) for k in range(3)]
        rstd = [sb(f"rstd{k}", [P, NI], F32) for k in range(3)]
        zero_row = sb("zero_row", [ROW // 6, 6], F32)
        mhalf = sb("mhalf", [P, NI], F32)
        aff = sb("aff", [P, NI, E], F32)
        top = sb("top", [P, NI, 8], F32)
        topi = sb("topi", [P, NI, 8], U32)
        topf = sb("topf", [P, NI], F32)
        ealpha = sb("ealpha", [P, NI], F32)
        ealpha1 = sb("ealpha1", [P, NI], F32)
        attn_end = place[0]

        place[0] = common_end
        b2_all = sb("b2_all", [P, E, D], F32)
        b1_col = sb("b1_col", [P, E, FC], F32)
        g_col = sb("g_col", [P, E, KC], F32)
        b_col = sb("b_col", [P, E, KC], F32)
        w12 = sb("w12", [P, E, KC * F + FC * D], F32)
        row_in = sb("row_in", [P, 6, ROW], F32)
        row_out = sb("row_out", [P, 3, D], F32)
        ht = sb("ht", [P, 2, KC, P], F32)
        h1 = sb("h1", [P, 2, F], F32)
        h1t = sb("h1t", [P, 2, FC, P], F32)
        yb = sb("yb", [P, 2, D], F32)
        ffn_end = place[0]
        place[0] = routing_at
        tot = sb("tot", [P, E, NT], F32)
        cum = sb("cum", [P, E, NT], F32)
        cnt = sb("cnt", [P, E], F32)
        cnt_i = sb("cnt_i", [P, E], I32)
        tiles_i = sb("tiles_i", [P, E], I32)
        tiles_f = sb("tiles_f", [P, E], F32)
        tiles_cum = sb("tiles_cum", [P, E], F32)
        adj = sb("adj", [P, E], F32)
        adj2 = sb("adj2", [P, E], F32)
        pos = sb("pos", [P, NT, E], F32)
        slot = sb("slot", [P, NT], F32)
        slot_i = sb("slot_i", [P, NT], I32)
        hi_i = sb("hi_i", [P, NT], I32)
        lo_i = sb("lo_i", [P, NT], I32)
        below = sb("below", [P, NS, E], F32)
        below_n = sb("below_n", [P, NS], F32)
        hot_lo = sb("hot_lo", [P, 8, P], F32)
        hot_hi = sb("hot_hi", [P, 8, NS], F32)

        assert place[0] <= routing_end
        bank = [ctx.enter_context(nc.psum_tensor(f"bank{n}", [P, 512], F32)) for n in range(8)]
        PP = bank[0:2]
        SB = bank[2:4]
        PT = bank[4:7]
        OB = bank[7]
        FZ, FH, FT, FY = bank[0], bank[1:3], bank[3:5], bank[5:7]

        s_const = sem("const_loaded")
        s_wraw = sem("w_raw_loaded")
        s_wsmall = sem("w_small_loaded")
        s_whead = sem("w_head_made")
        s_wrest = sem("w_rest_made")
        s_cb = sem("bf16_consts_made")
        s_xa = sem("xa_loaded")
        s_xr = sem("xr_loaded")
        s_xmean = sem("x_stats_made")
        s_xrstd = sem("x_rstd_made")
        s_xveps = sem("x_veps_made")
        s_xh = sem("xh_made")
        s_ppdone = sem("pp_written")
        s_ppread = sem("pp_read")
        s_xth = sem("xt_head_made")
        s_vh = sem("v_head_made")
        s_swap = sem("halves_swapped")
        s_qsin = sem("q_times_sin_made")
        s_kprod = sem("k_products_made")
        s_rope = sem("rope_summed")
        s_qkh = sem("qk_head_made")
        s_qkl = sem("qk_rest_made")
        s_score = sem("scores_written")
        s_max = sem("max_made")
        s_exp = sem("exp_made")
        s_rden = sem("rdenom_made")
        s_pscaled = sem("probs_scaled")
        s_ptdone = sem("pt_written")
        s_pth = sem("pt_head_made")
        s_ptl = sem("pt_rest_made")
        s_obdone = sem("ob_written")
        s_obread = sem("ob_read")
        s_dve = sem("dve_step")
        s_own = [sem(n) for n in ("x_bn_made", "x1_bn_made", "xn_bn_made", "top_index_made", "top_float_made",
                                  "exp_plus_one_made")]
        s_nstat = sem("x1_stats_made")
        s_nveps = sem("x1_veps_made")
        s_nrstd = sem("x1_rstd_made")
        s_xn = sem("xn_made")
        s_zstat = sem("xn_stats_made")
        s_zveps = sem("xn_veps_made")
        s_zrstd = sem("xn_rstd_made")
        s_skip = sem("skip_made")
        s_z = sem("z_made")
        s_top = sem("top_made")
        s_ea = sem("exp_neg_top_made")
        s_gate = sem("gate_made")
        s_rows = sem("rows_stored")
        s_zrow = sem("zero_row_made")
        s_half = sem("mhalf_made")

        s_hot = sem("onehots_made")
        s_count = sem("counts_written")
        s_hhi = sem("slot_tile_hot_made")
        s_route = sem("slot_hot_made")
        s_routeb = sem("slot_hot_used")
        s_ids = sem("slot_tok_written")
        s_idx = sem("slot_tok_made")
        s_texp = sem("tile_exp_made")

        s_fw = sem("ffn_weights_loaded")
        s_gat = [sem(f"row_gathered{k}") for k in range(6)]
        s_sca = [sem(f"row_scattered{k}") for k in range(3)]
        s_passed = sem("wait_passed")
        s_now = sem("tok_now_made")
        s_zt = sem("zt_written")
        s_ht = sem("ht_made")
        s_h1 = sem("h1_written")
        s_h1a = sem("h1_read_by_act")
        s_h1d = sem("h1_read_by_dve")
        s_hT = sem("h1t_written")
        s_hTa = sem("h1t_read_by_act")
        s_hTd = sem("h1t_read_by_dve")
        s_y = sem("y_written")
        s_yb = sem("y_biased")
        s_comb = sem("row_combined")

        PPN = lambda b: 14 + 30 * b
        UN = lambda b: 4 + 16 * b
        obn = lambda b: 11 * b

        def unit_at(b, h):
            k = h if h < 7 else h - 1
            return UN(b) + 2 * k, PPN(b) + 2 * h, (k + 2) % 4

        def has_units(h, last):
            return h < 6 or (h > 6 and not last)

        def split_k(h, last):
            return h != 7 and (h != 8 or not last)

        ROWS = lambda b: 16 + 48 * b

        x_v = x.rearrange("b (i p) d -> b p i d", p=P)
        rows_v = tok_rows[0:B * T, :].rearrange("(b i p) r -> b p i r", p=P, i=NI)
        out_v = out.rearrange("b t d -> (b t) d")

        block = ctx.enter_context(nc.Block())

        def passed(eng):
            eng.sem_inc(s_passed, 1)

        @block.sync
        def _(sp):
            sp.dma_start(cst[:, :], consts).then_inc(s_const, 16)
            sp.dma_start(xa[:, :, :], x_v[0]).then_inc(s_xa, 16)
            for n, w in ((0, w_q), (1, w_k), (2, w_v)):
                sp.dma_start(w_raw[:, n, :, :], w.rearrange("(c p) n -> p c n", p=P)).then_inc(s_wraw, 16)
            sp.dma_start(wo[:, :, :], w_o.rearrange("(h p) n -> p h n", p=P)).then_inc(s_wsmall, 16)
            sp.dma_start(cent[:, :, :], cent_t.rearrange("(c p) e -> p c e", p=P)).then_inc(s_wsmall, 16)
            sp.dma_start(xr[:, :, :], x_v[0]).then_inc(s_xr, 16)
            sp.wait_ge(s_xh, 1)
            sp.dma_start(xa[:, :, :], x_v[1]).then_inc(s_xa, 16)
            sp.wait_ge(s_zrow, 1)
            sp.dma_start(tok_rows[B * T:B * T + 1, :].rearrange("o (p c) -> (o p) c", c=6), zero_row[:, :]).then_inc(s_rows, 16)
            sp.wait_ge(s_rows, 16)

            def store_rows(b):
                place_b = rows_v[bass.ds(b, 1)].rearrange("o p i r -> (o p) i r")
                sp.wait_ge(s_skip, 1 * (b + 1))
                passed(sp)
                sp.dma_start(place_b[:, :, D:2 * D], x1[:, :, :]).then_inc(s_rows, 16)
                sp.wait_ge(s_z, 1 * (b + 1))
                passed(sp)
                sp.dma_start(place_b[:, :, 0:D], xn[:, :, :]).then_inc(s_rows, 16)
                sp.wait_ge(s_gate, 1 * (b + 1))
                passed(sp)
                sp.dma_start(place_b[:, :, 2 * D:ROW], gates[:, :, :]).then_inc(s_rows, 16)

            def load_xr(b):
                sp.wait_ge(s_ppread, PPN(b) - 6)
                sp.dma_start(xr[:, :, :], x_v[bass.ds(b, 1)].rearrange("o p i d -> (o p) i d")).then_inc(s_xr, 16)

            def load_xa(b):
                sp.wait_ge(s_xh, b)
                sp.dma_start(xa[:, :, :], x_v[bass.ds(b, 1)].rearrange("o p i d -> (o p) i d")).then_inc(s_xa, 16)

            with sp.Fori(1, B - 1) as b:
                load_xa(b + 1)
                load_xr(b)
                store_rows(b - 1)
            load_xr(B - 1)
            store_rows(B - 2)

            def load_expert(e):
                sp.dma_start(w12[:, e, 0:KC * F].rearrange("p (c f) -> p c f", c=KC),
                             w1_t[e].rearrange("(c p) f -> p c f", p=P)).then_inc(s_fw, 16)
                sp.dma_start(w12[:, e, KC * F:KC * F + FC * D].rearrange("p (c d) -> p c d", c=FC),
                             w2_t[e].rearrange("(c p) d -> p c d", p=P)).then_inc(s_fw, 16)

            sp.wait_ge(s_ppdone, PPN(B - 1) + 12)
            for t, src in ((g_col, ln_g), (b_col, ln_b)):
                sp.dma_start(t[:, :, :], src.rearrange("e (c p) -> p e c", p=P),
                             allow_slow_non_contiguous=True).then_inc(s_fw, 16)
            sp.dma_start(b1_col[:, :, :], b1.rearrange("e (c p) -> p e c", p=P),
                         allow_slow_non_contiguous=True).then_inc(s_fw, 16)
            sp.dma_start(b2_all[:, :, :].rearrange("p e d -> p (e d)"),
                         b2.rearrange("e d -> (e d)").rearrange("(o n) -> o n", o=1).broadcast_to([P, E * D])
                         ).then_inc(s_fw, 16)
            for e in range(3):
                load_expert(e)
            sp.wait_ge(s_score, 32 * B)
            load_expert(3)
            sp.wait_ge(s_ptdone, 24 * B)
            load_expert(4)
            sp.wait_ge(s_ppread, PPN(B - 1) + 16)
            load_expert(5)
            load_expert(6)
            load_expert(7)
            store_rows(B - 1)

        FW = 16 * (4 + 2 * E)

        @block.gpsimd
        def _(pool):
            pool.memset(mhalf[:, :], -0.5).then_inc(s_half, 1)
            pool.memset(ones_b[:, :], 1.0).then_inc(s_cb, 1)
            pool.memset(ones_f[:, :], 1.0).then_inc(s_cb, 1)
            pool.memset(zero_row[:, :], 0.0).then_inc(s_zrow, 1)
            pool.memset(gates[:, :, 1:ROW - 2 * D], 0.0).then_inc(s_half, 1)
            pool.wait_ge(s_half, 2)

            def power(k, stat, made, done, n):
                pool.wait_ge(stat, n + 1)
                passed(pool)
                pool.tensor_scalar(veps[k][:, :], mv[k][:, :, 1], EPS, None, ALU.add).then_inc(made, 1)
                pool.wait_ge(made, n + 1)
                pool.tensor_tensor(rstd[k][:, :], veps[k][:, :], mhalf[:, :], ALU.pow).then_inc(done, 1)

            def rope_sum(n, g, kind):
                if kind == 0:
                    pool.wait_ge(s_swap, n + 1)
                    pool.tensor_tensor(rope_s[:, 0, :], rope_s[:, 0, :], cst[:, C_SIN:C_SIN + T],
                                       ALU.mult).then_inc(s_qsin, 2)
                    pool.wait_ge(s_qsin, n + 2)
                    pool.wait_ge(s_ppread, g + 1)
                else:
                    pool.wait_ge(s_kprod, n + 2)
                pool.tensor_tensor(rope_c[:, kind, :], rope_c[:, kind, :], rope_s[:, kind, :],
                                   ALU.add).then_inc(s_rope, 1)

            def qk_rest(n, par, kind):
                pool.wait_ge(s_qkh, n + kind + 1)
                pool.tensor_tensor(qkl[:, par, kind, :], rope_c[:, kind, :], qkh[:, par, kind, :].bitcast(F32),
                                   ALU.subtract).then_inc(s_qkl, 1)

            def skip(b):
                pool.wait_ge(s_xn, b + 1)
                pool.tensor_tensor(x1[:, :, :], x1[:, :, :], xn[:, :, :], ALU.add).then_inc(s_skip, 1)

            def batch(b, first=False, last=False):
                for h in range(H + 1):
                    n, g, par = unit_at(b, h)
                    if split_k(h, last):
                        qk_rest(n - 2, (par - 1) % 4, 1)
                    if has_units(h, last):
                        rope_sum(n, g, 0)
                        qk_rest(n, par, 0)
                        rope_sum(n, g, 1)
                    if h == 2 and not last:
                        power(0, s_xmean, s_xveps, s_xrstd, b + 1)
                power(1, s_nstat, s_nveps, s_nrstd, b)
                skip(b)
                power(2, s_zstat, s_zveps, s_zrstd, b)

            power(0, s_xmean, s_xveps, s_xrstd, 0)
            rope_sum(0, 2, 0)
            qk_rest(0, 0, 0)
            rope_sum(0, 2, 1)
            qk_rest(0, 0, 1)
            rope_sum(2, 4, 0)
            qk_rest(2, 1, 0)
            rope_sum(2, 4, 1)
            batch(0, first=True)
            with pool.Fori(1, B - 1) as b:
                batch(b)
            batch(B - 1, last=True)

            pool.wait_ge(s_rows, ROWS(B))
            pool.wait_ge(s_idx, 1)

            def gather(j, k, again=None):
                if again is not None:
                    pool.wait_ge(s_sca[k % 3], 16 * again)
                pool.tensor_copy(tok_now[:, k % 6:k % 6 + 1], slot_tok[:, bass.ds(j, 1)]).then_inc(s_now, 1)
                pool.wait_ge(s_now, j + 1)
                passed(pool)
                pool.indirect_dma_start(row_in[:, k % 6, :], None, tok_rows,
                                        bass.IndirectOffsetOnAxis(ap=tok_now[:, k % 6:k % 6 + 1], axis=0)
                                        ).then_inc(s_gat[k % 6], 16)

            def scatter(j, k):
                pool.wait_ge(s_comb, j + 1)
                passed(pool)
                pool.indirect_dma_start(out_v, bass.IndirectOffsetOnAxis(ap=tok_now[:, k % 6:k % 6 + 1], axis=0),
                                        row_out[:, k % 3, :], None, bounds_check=B * T - 1, oob_is_err=False
                                        ).then_inc(s_sca[k % 3], 16)

            for j in range(5):
                gather(j, j)
            for j in range(6):
                scatter(j, j)
                gather(j + 5, j + 5, None if j == 0 else (j - 1) // 3 + 1)
            with pool.Fori(1, NS // 6 - 1) as it:
                for k in range(6):
                    scatter(6 * it + k, k)
                    gather(6 * it + k + 5, k + 5, 2 * it + (k - 1) // 3 + 1)
            for j in range(NS // 6 * 6 - 6, NS):
                scatter(j, j)
                if j + 5 < NS:
                    gather(j + 5, j + 5, (j - 1) // 3 + 1)
            for k in range(3):
                pool.wait_ge(s_sca[k], 16 * (NS // 3))

        @block.scalar
        def _(act):
            act.wait_ge(s_const, 16)
            act.activation(ident_b[:, :], ident, ACT.Copy).then_inc(s_cb, 1)
            act.activation(mask_b[:, :], cst[:, C_MASK:C_MASK + P], ACT.Copy).then_inc(s_cb, 1)
            act.activation(lower_b[:, :], cst[:, C_LT:C_LT + P], ACT.Copy).then_inc(s_cb, 1)
            act.wait_ge(s_wraw, 48)
            for n in range(3):
                for c in range(KC):
                    act.activation(wh[:, n, c, :], w_raw[:, n, c, :], ACT.Copy,
                                   scale=1.0 / DH if n == 0 else 1.0).then_inc(s_whead, 1)

            def xt_head(g):
                for c in range(KC):
                    act.wait_ge(s_ppdone, g + c + 1)
                    act.activation(xth[:, c, :], PP[c][:, :], ACT.Copy).then_inc(s_xth, 1)

            def v_head(g, m):
                act.wait_ge(s_ppdone, g + 1)
                act.activation(vh[:, m // 2, (m % 2) * 512:(m % 2) * 512 + 512], PP[m % 2][:, :],
                               ACT.Copy).then_inc(s_vh, 1)

            def swap(n, g, kind):
                act.wait_ge(s_ppdone, g + kind + 1)
                if not (isinstance(n, int) and n + kind < 2):
                    act.wait_ge(s_rope, n + kind - 1)
                act.activation(rope_s[0:64, kind, :], PP[kind][64:128, :], ACT.Copy)
                act.activation(rope_s[64:128, kind, :], PP[kind][0:64, :], ACT.Copy).then_inc(s_swap, 1)

            def qk_head(n, par, kind):
                act.wait_ge(s_rope, n + kind + 1)
                act.activation(qkh[:, par, kind, :], rope_c[:, kind, :], ACT.Copy).then_inc(s_qkh, 1)

            def exps(b, h, i):
                n = 32 * b + 4 * h + i
                act.wait_ge(s_max, n + 1)
                act.activation(prob[:, h % 2, POFF[i]:POFF[i] + (i + 1) * P], SB[i % 2][:, 0:(i + 1) * P], ACT.Exp,
                               bias=negmax[:, h % 2, i:i + 1], scale=1.0,
                               accum_out=denom[:, h % 2, i:i + 1]).then_inc(s_exp, 1)

            def pt_head(b, h, c):
                act.wait_ge(s_ptdone, 24 * b + 3 * h + c + 1)
                lo, w = CHUNK[c]
                act.activation(pth[:, lo:lo + w], PT[c][:, 0:w], ACT.Copy).then_inc(s_pth, 1)

            def o_out(b, h):
                act.wait_ge(s_obdone, obn(b) + h + 1)
                act.activation(ot[:, h, :], OB[:, :], ACT.Copy).then_inc(s_obread, 1)

            def xn_out(n, c):
                act.wait_ge(s_obdone, n + 1)
                act.activation(xnt[:, c, :], OB[:, :], ACT.Copy).then_inc(s_obread, 1)

            def aff_out(n):
                act.wait_ge(s_obdone, n + 1)
                act.activation(aff[:, :, :], OB[:, 0:NI * E].rearrange("p (i e) -> p i e", i=NI),
                               ACT.Copy).then_inc(s_obread, 1)

            def gate_exp(b):
                act.wait_ge(s_top, b + 1)
                act.activation(ealpha[:, :], top[:, :, 0], ACT.Exp, scale=-1.0).then_inc(s_ea, 1)

            def batch(b, last=False):
                ob = obn(b)
                for h in range(H + 1):
                    n, g, par = unit_at(b, h)
                    unit = has_units(h, last)
                    if h < H:
                        exps(b, h, 0)
                    if h >= 2:
                        o_out(b, h - 2)
                    if h < H:
                        exps(b, h, 1)
                    if split_k(h, last):
                        qk_head(n - 2, (par - 1) % 4, 1)
                    if unit:
                        swap(n, g, 0)
                    if h == 6 and not last:
                        xt_head(g)
                    if h < H:
                        exps(b, h, 2)
                    if h >= 1:
                        for c in range(3):
                            pt_head(b, h - 1, c)
                    if unit:
                        swap(n, g, 1)
                    if unit and h > 0:
                        qk_head(n, par, 0)
                    if h < H:
                        exps(b, h, 3)
                    if h == 0:
                        qk_head(n, par, 0)
                    if h == 3 and not (isinstance(b, int) and b == 0):
                        gate_exp(b - 1)
                o_out(b, H - 1)
                if last:
                    xn_out(ob + 8, 0)
                    xn_out(ob + 9, 1)
                    aff_out(ob + 10)
                else:
                    for m in range(2 * NI):
                        v_head(PPN(b) + 18 + m + (0 if m < 2 else NI), m)
                        if m == 4:
                            xn_out(ob + 8, 0)
                        if m == 5:
                            xn_out(ob + 9, 1)
                        if m == 6:
                            aff_out(ob + 10)

            xt_head(0)
            swap(0, 2, 0)
            swap(0, 2, 1)
            qk_head(0, 0, 0)
            qk_head(0, 0, 1)
            swap(2, 4, 0)
            swap(2, 4, 1)
            v_head(6, 0)
            v_head(7, 1)
            qk_head(2, 1, 0)
            for m in range(2, 2 * NI):
                v_head(6 + m, m)
            batch(0)
            with act.Fori(1, B - 1) as b:
                batch(b)
            batch(B - 1, last=True)
            gate_exp(B - 1)

            def h1_out(j, k):
                act.wait_ge(s_h1, 2 * j + 1)
                act.activation(h1[:, k % 2, 0:512], FH[0][:, :], ACT.Copy).then_inc(s_h1a, 1)

            def h1t_out(j, k, e):
                act.wait_ge(s_hT, 2 * j + 1)
                for c in range(4):
                    ins = act.activation(h1t[:, k % 2, c, :], FT[0][:, c * P:(c + 1) * P], ACT.Relu,
                                         bias=b1_col[:, bass.ds(e, 1), c:c + 1].rearrange("p a b -> p (a b)"),
                                         scale=1.0)
                ins.then_inc(s_hTa, 1)

            act.wait_ge(s_texp, 1)
            act.wait_ge(s_fw, FW)

            def tile(j, k):
                e = act.value_load(tile_exp[0:1, bass.ds(j, 1)], min_val=0, max_val=E - 1)
                h1_out(j, k)
                h1t_out(j, k, e)

            with act.Fori(0, NS // 6) as it:
                for k in range(6):
                    tile(6 * it + k, k)
            for j in range(NS - 3, NS):
                tile(j, j)

        @block.tensor
        def _(pe):
            def mm3(out_ap, lh, ll, rh, rl, start, stop):
                pe.matmul(out_ap, ll, rh, start=start, stop=False)
                pe.matmul(out_ap, lh, rl, start=False, stop=False)
                return pe.matmul(out_ap, lh, rh, start=False, stop=stop)

            def pp_free(g):
                if not (isinstance(g, int) and g < 2):
                    pe.wait_ge(s_ppread, g - 1)

            def xt(b, g):
                pe.wait_ge(s_xh, b + 1)
                for c in range(KC):
                    pp_free(g + c)
                    for i in range(NI):
                        mm = pe.transpose(PP[c][:, i * P:(i + 1) * P], xh[:, i, c * P:(c + 1) * P], ident)
                    mm.then_inc(s_ppdone, 1)

            def unit_project(g, kind, head, new_batch=False):
                if new_batch:
                    pe.wait_ge(s_ppread, g)
                else:
                    pp_free(g)
                for c in range(KC):
                    mm = mm3(PP[kind][:, :], wh[:, kind, c, head * DH:(head + 1) * DH],
                             wl[:, kind, c, head * DH:(head + 1) * DH], xth[:, c, :], xtl[:, c, :],
                             c == 0, c == KC - 1)
                mm.then_inc(s_ppdone, 1)

            def v_project(g, m):
                pp_free(g)
                i, half = m // 2, m % 2
                for c in range(KC):
                    mm = mm3(PP[m % 2][:, :], xth[:, c, i * P:(i + 1) * P], xtl[:, c, i * P:(i + 1) * P],
                             wh[:, 2, c, half * 512:half * 512 + 512], wl[:, 2, c, half * 512:half * 512 + 512],
                             c == 0, c == KC - 1)
                mm.then_inc(s_ppdone, 1)

            def score(b, h, i):
                if i == 0:
                    pe.wait_ge(s_qkl, 16 * b + 2 * h + 2)
                n = 32 * b + 4 * h + i
                if not (isinstance(b, int) and n < 2):
                    pe.wait_ge(s_exp, n - 1)
                w = (i + 1) * P
                par = h % 4
                mm3(SB[i % 2][:, 0:w], qkh[:, par, 0, i * P:(i + 1) * P], qkl[:, par, 0, i * P:(i + 1) * P],
                    qkh[:, par, 1, 0:w], qkl[:, par, 1, 0:w], True, False)
                pe.matmul(SB[i % 2][:, i * P:w], ident_b[:, :], mask_b[:, :],
                          start=False, stop=True).then_inc(s_score, 1)

            def turn_probs(b, h, c):
                if c == 0:
                    pe.wait_ge(s_pscaled, 8 * b + h + 1)
                if not (isinstance(b, int) and b == 0 and h == 0):
                    pe.wait_ge(s_ptl, 24 * b + 3 * h + c - 2)
                for j in ((0,), (1,), (2, 3))[c]:
                    for i in range(j, NI):
                        o = TOFF[j] - CHUNK[c][0] + (i - j) * P
                        mm = pe.transpose(PT[c][:, o:o + P], prob[:, h % 2, POFF[i] + j * P:POFF[i] + (j + 1) * P],
                                          ident)
                mm.then_inc(s_ptdone, 1)

            def ob_free(n):
                if not (isinstance(n, int) and n == 0):
                    pe.wait_ge(s_obread, n)

            def attend(b, h):
                if h == 0:
                    pe.wait_ge(s_ppread, PPN(b))
                ob_free(obn(b) + h)
                for j in range(NI):
                    if j < 3:
                        pe.wait_ge(s_ptl, 24 * b + 3 * h + j + 1)
                    at = slice(TOFF[j], TOFF[j] + (NI - j) * P)
                    mm = mm3(OB[:, j * P:T], vh[:, j, h * P:(h + 1) * P], vl[:, j, h * P:(h + 1) * P],
                             pth[:, at], ptl[:, at], j == 0, j == NI - 1)
                mm.then_inc(s_obdone, 1)

            def out_project(b, g, i):
                if i == 0:
                    pe.wait_ge(s_obread, obn(b) + H)
                pp_free(g)
                for h in range(H):
                    mm = pe.matmul(PP[i % 2][:, 0:D], ot[:, h, i * P:(i + 1) * P], wo[:, h, :],
                                   start=(h == 0), stop=(h == H - 1))
                mm.then_inc(s_ppdone, 1)

            def xn_turn(b, n, c):
                if c == 0:
                    pe.wait_ge(s_xn, b + 1)
                ob_free(n)
                for i in range(NI):
                    mm = pe.transpose(OB[:, i * P:(i + 1) * P], xn[:, i, c * P:(c + 1) * P], ident)
                mm.then_inc(s_obdone, 1)

            def affinity(n):
                ob_free(n)
                for i in range(NI):
                    for c in range(KC):
                        mm = pe.matmul(OB[:, i * E:(i + 1) * E], xnt[:, c, i * P:(i + 1) * P], cent[:, c, :],
                                       start=(c == 0), stop=(c == KC - 1))
                mm.then_inc(s_obdone, 1)

            def batch(b, last=False):
                ob, pp = obn(b), PPN(b)
                for h in range(H + 1):
                    _, g, _ = unit_at(b, h)
                    unit = has_units(h, last)
                    head = h + 2 if h < 6 else h - 7
                    if h < H:
                        score(b, h, 0)
                    if h >= 2:
                        attend(b, h - 2)
                    if h < H:
                        score(b, h, 1)
                    if unit:
                        unit_project(g, 0, head, h == 7)
                    if h == 6 and not last:
                        xt(b + 1, g)
                    if h < H:
                        score(b, h, 2)
                    if h >= 1:
                        for c in range(3):
                            turn_probs(b, h - 1, c)
                    if unit:
                        unit_project(g + 1, 1, head)
                    if h < H:
                        score(b, h, 3)
                if not last:
                    v_project(pp + 18, 0)
                attend(b, H - 1)
                if not last:
                    v_project(pp + 19, 1)
                o0 = pp + (20 if not last else 12)
                for i in range(NI):
                    out_project(b, o0 + i, i)
                if last:
                    xn_turn(b, ob + 8, 0)
                    xn_turn(b, ob + 9, 1)
                    affinity(ob + 10)
                else:
                    for m in range(2, 2 * NI):
                        v_project(pp + 22 + m, m)
                        if m == 4:
                            xn_turn(b, ob + 8, 0)
                        if m == 5:
                            xn_turn(b, ob + 9, 1)
                        if m == 6:
                            affinity(ob + 10)

            pe.wait_ge(s_const, 16)
            xt(0, 0)
            pe.wait_ge(s_wrest, 6)
            unit_project(2, 0, 0, True)
            unit_project(3, 1, 0)
            unit_project(4, 0, 1)
            unit_project(5, 1, 1)
            for m in range(2 * NI):
                v_project(6 + m, m)
            pe.wait_ge(s_cb, 5)
            pe.wait_ge(s_wsmall, 32)
            batch(0)
            with pe.Fori(1, B - 1) as b:
                batch(b)
            batch(B - 1, last=True)

            pe.wait_ge(s_hot, B)
            oh = onehot[:, :, :].rearrange("p t e -> p (t e)")
            pe.matmul(SB[0][:, 0:NT * E], lower_b[:, :], oh, start=True, stop=True)
            pe.matmul(SB[1][:, 0:NT * E], ones_b[:, :], oh, start=True, stop=True).then_inc(s_count, 1)
            for t in range(NT):
                if t % 4 == 0:
                    pe.wait_ge(s_route, t // 4 + 1)
                mm = pe.matmul(PT[0][:, 0:NS], hot_lo[:, t % 8, :], hot_hi[:, t % 8, :],
                               start=(t == 0), stop=(t == NT - 1))
                if t % 4 == 3:
                    mm.then_inc(s_routeb, 1)

            def turn_z(j, k, used):
                pe.wait_ge(s_gat[k % 6], 16 * used + 16)
                if not (isinstance(j, int) and j == 0):
                    pe.wait_ge(s_ht, j)
                for c in range(KC):
                    mm = pe.transpose(FZ[:, c * P:(c + 1) * P], row_in[:, k % 6, c * P:(c + 1) * P], ident)
                mm.then_inc(s_zt, 1)

            def up(j, k, e):
                pe.wait_ge(s_ht, j + 1)
                if not (isinstance(j, int) and j == 0):
                    pe.wait_ge(s_h1a, j)
                for half in range(2):
                    if half == 1 and not (isinstance(j, int) and j == 0):
                        pe.wait_ge(s_h1d, j)
                    for c in range(KC):
                        mm = pe.matmul(FH[half][:, :], ht[:, k % 2, c, :],
                                       w12[:, bass.ds(e, 1), c * F + half * 512:c * F + half * 512 + 512
                                           ].rearrange("p o f -> p (o f)"),
                                       start=(c == 0), stop=(c == KC - 1))
                    mm.then_inc(s_h1, 1)

            def turn_h(j, k):
                for half in range(2):
                    if half == 0:
                        pe.wait_ge(s_h1a, j + 1)
                    else:
                        pe.wait_ge(s_h1d, j + 1)
                    if not (isinstance(j, int) and j == 0):
                        pe.wait_ge(s_hTa if half == 0 else s_hTd, j)
                    for c in range(4):
                        mm = pe.transpose(FT[half][:, c * P:(c + 1) * P],
                                          h1[:, k % 2, half * 512 + c * P:half * 512 + (c + 1) * P], ident)
                    mm.then_inc(s_hT, 1)

            def down(j, k, e):
                if not (isinstance(j, int) and j == 0):
                    pe.wait_ge(s_yb, j)
                for c in range(FC):
                    if c == 0:
                        pe.wait_ge(s_hTa, j + 1)
                    if c == 4:
                        pe.wait_ge(s_hTd, j + 1)
                    mm = pe.matmul(FY[k % 2][:, 0:D], h1t[:, k % 2, c, :],
                                   w12[:, bass.ds(e, 1), KC * F + c * D:KC * F + (c + 1) * D
                                       ].rearrange("p o d -> p (o d)"),
                                   start=(c == 0), stop=(c == FC - 1))
                mm.then_inc(s_y, 1)

            pe.wait_ge(s_texp, 1)
            pe.wait_ge(s_fw, FW)

            def expert(j):
                return pe.value_load(tile_exp[0:1, bass.ds(j, 1)], min_val=0, max_val=E - 1)

            e0 = expert(0)
            turn_z(0, 0, 0)
            up(0, 0, e0)
            e1 = expert(1)
            turn_h(0, 0)
            turn_z(1, 1, 0)

            def step(j, k, used, e_j, e_next):
                up(j + 1, k + 1, e_next)
                turn_z(j + 2, k + 2, used)
                down(j, k, e_j)
                e_after = expert(j + 2)
                turn_h(j + 1, k + 1)
                return e_next, e_after

            for j in range(3):
                e0, e1 = step(j, j, (j + 2) // 6, e0, e1)
            with pe.Fori(0, NS // 6 - 1) as it:
                ea, eb = expert(6 * it + 3), expert(6 * it + 4)
                for k in range(6):
                    ea, eb = step(6 * it + 3 + k, 3 + k, it + (k + 5) // 6, ea, eb)
            e0, e1 = expert(NS - 6), expert(NS - 5)
            for j in range(NS - 6, NS - 2):
                e0, e1 = step(j, j, (j + 2) // 6, e0, e1)
            up(NS - 1, NS - 1, e1)
            down(NS - 2, NS - 2, e0)
            turn_h(NS - 1, NS - 1)
            down(NS - 1, NS - 1, e1)

        @block.vector
        def _(dve):
            def norm_stats(k, src, made):
                for i in range(NI):
                    ins = dve.bn_stats(stats[k][:, i, :], src[:, i, :])
                ins.then_inc(made, 1)

            def norm_aggr(k, own, n, made):
                dve.wait_ge(own, n)
                passed(dve)
                for i in range(NI):
                    ins = dve.bn_aggr(mv[k][:, i, :], stats[k][:, i, :])
                ins.then_inc(made, 1)

            def norm_apply(k, dst, src, rdy, n, made):
                dve.wait_ge(rdy, n)
                for i in range(NI):
                    ins = dve.tensor_scalar(dst[:, i, 0:D], src[:, i, :], mv[k][:, i, 0:1], rstd[k][:, i:i + 1],
                                            ALU.subtract, ALU.mult)
                ins.then_inc(made, 1)

            def ln_x_stats(b):
                dve.wait_ge(s_xa, 16 * (b + 1))
                norm_stats(0, xa, s_lnx)
                norm_aggr(0, s_lnx, b + 1, s_xmean)

            def ln_x(b, g):
                if g is not None:
                    dve.wait_ge(s_ppdone, g)
                norm_apply(0, xh, xa, s_xrstd, b + 1, s_xh)

            def xt_rest(b):
                for c in range(KC):
                    dve.wait_ge(s_xth, 2 * b + c + 1)
                    dve.tensor_tensor(xtl[:, c, :], PP[c][:, :], xth[:, c, :].bitcast(F32),
                                      ALU.subtract).then_inc(s_ppread, 1)

            def times_cos(n, kind):
                dve.wait_ge(s_swap, n + kind + 1)
                if not (isinstance(n, int) and n + kind < 2):
                    dve.wait_ge(s_qkl, n + kind - 1)
                dve.tensor_tensor(rope_c[:, kind, :], PP[kind][:, :], cst[:, C_COS:C_COS + T],
                                  ALU.mult).then_inc(s_ppread, 1)

            def k_products(n):
                times_cos(n, 1)
                dve.tensor_tensor(rope_s[:, 1, :], rope_s[:, 1, :], cst[:, C_SIN:C_SIN + T],
                                  ALU.mult).then_inc(s_kprod, 2)

            def v_rest(b, m):
                dve.wait_ge(s_vh, 8 * b + m + 1)
                at = slice((m % 2) * 512, (m % 2) * 512 + 512)
                dve.tensor_tensor(vl[:, m // 2, at], PP[m % 2][:, :], vh[:, m // 2, at].bitcast(F32),
                                  ALU.subtract).then_inc(s_ppread, 1)

            def row_max(b, h, i):
                n = 32 * b + 4 * h + i
                dve.wait_ge(s_score, n + 1)
                dve.tensor_reduce(negmax[:, h % 2, i:i + 1], SB[i % 2][:, 0:(i + 1) * P], AX.X, ALU.max,
                                  negate=True).then_inc(s_max, 1)

            def scale_probs(b, h):
                dve.wait_ge(s_exp, 32 * b + 4 * h + 4)
                dve.reciprocal(rdenom[:, h % 2, :], denom[:, h % 2, :]).then_inc(s_rden, 1)
                dve.wait_ge(s_rden, 8 * b + h + 1)
                for i in range(NI):
                    p_i = prob[:, h % 2, POFF[i]:POFF[i] + (i + 1) * P]
                    ins = dve.tensor_scalar(p_i, p_i, rdenom[:, h % 2, i:i + 1], None, ALU.mult)
                ins.then_inc(s_pscaled, 1)

            def pt_rest(b, h, c):
                dve.wait_ge(s_pth, 24 * b + 3 * h + c + 1)
                lo, w = CHUNK[c]
                dve.tensor_tensor(ptl[:, lo:lo + w], PT[c][:, 0:w], pth[:, lo:lo + w].bitcast(F32),
                                  ALU.subtract).then_inc(s_ptl, 1)

            def residual(b, g, i):
                if i == 0:
                    dve.wait_ge(s_xr, 16 * (b + 1))
                dve.wait_ge(s_ppdone, g + 1)
                dve.tensor_tensor(x1[:, i, :], PP[i % 2][:, 0:D], xr[:, i, :], ALU.add).then_inc(s_ppread, 1)

            def choose(b):
                passed(dve)
                for i in range(NI):
                    ins = dve.max(top[:, i, :], aff[:, i, :])
                ins.then_inc(s_top, 1)
                dve.wait_ge(s_top, b + 1)
                passed(dve)
                for i in range(NI):
                    ins = dve.max_index(topi[:, i, :], top[:, i, :], aff[:, i, :])
                ins.then_inc(s_topi, 1)
                dve.wait_ge(s_topi, b + 1)
                dve.tensor_copy(topf[:, :], topi[:, :, 0]).then_inc(s_topf, 1)
                dve.wait_ge(s_topf, b + 1)
                dve.tensor_tensor(onehot[:, bass.ds(NI * b, NI), :],
                                  cst[:, C_IOTA:C_IOTA + E].rearrange("p (o e) -> p o e", o=1).broadcast_to([P, NI, E]),
                                  topf[:, :].rearrange("p (i o) -> p i o", o=1).broadcast_to([P, NI, E]),
                                  ALU.is_equal).then_inc(s_hot, 1)

            def gate(b):
                dve.wait_ge(s_ea, b + 1)
                dve.tensor_scalar(ealpha1[:, :], ealpha[:, :], 1.0, None, ALU.add).then_inc(s_ea1, 1)
                dve.wait_ge(s_ea1, b + 1)
                dve.reciprocal(gates[:, :, 0], ealpha1[:, :]).then_inc(s_gate, 1)

            def between(b, h, first, last):
                if h == 1 and not last:
                    ln_x_stats(b + 1)
                if h == 2 and not first:
                    dve.wait_ge(s_obread, obn(b))
                    choose(b - 1)
                if h == 3 and not last:
                    ln_x(b + 1, PPN(b) - 16 if not first else 2)
                if h == 4 and not first:
                    gate(b - 1)

            def batch(b, first=False, last=False):
                pp = PPN(b)
                for h in range(H + 1):
                    n, g, _ = unit_at(b, h)
                    unit = has_units(h, last)
                    if h < H:
                        row_max(b, h, 0)
                        row_max(b, h, 1)
                    if h >= 1:
                        scale_probs(b, h - 1)
                    if h < H:
                        row_max(b, h, 2)
                    between(b, h, first, last)
                    if unit:
                        times_cos(n, 0)
                    if h == 6 and not last:
                        xt_rest(b + 1)
                    if h >= 1:
                        for c in range(3):
                            pt_rest(b, h - 1, c)
                    if h < H:
                        row_max(b, h, 3)
                    if unit:
                        k_products(n)
                if not last:
                    v_rest(b + 1, 0)
                    v_rest(b + 1, 1)
                if not first:
                    dve.wait_ge(s_rows, ROWS(b))
                o0 = pp + (20 if not last else 12)
                for i in range(NI):
                    residual(b, o0 + i, i)
                    dve.wait_ge(s_ppread, o0 + i + 1)
                    ins = dve.bn_stats(stats[1][:, i, :], x1[:, i, :])
                ins.then_inc(s_lnn, 1)
                norm_aggr(1, s_lnn, b + 1, s_nstat)
                if not last:
                    v_rest(b + 1, 2)
                norm_apply(1, xn, x1, s_nrstd, b + 1, s_xn)
                if not last:
                    v_rest(b + 1, 3)
                    v_rest(b + 1, 4)
                dve.wait_ge(s_xn, b + 1)
                norm_stats(2, xn, s_lnz)
                if not last:
                    v_rest(b + 1, 5)
                norm_aggr(2, s_lnz, b + 1, s_zstat)
                if not last:
                    v_rest(b + 1, 6)
                dve.wait_ge(s_obdone, obn(b) + 10)
                dve.wait_ge(s_skip, b + 1)
                norm_apply(2, xn, xn, s_zrstd, b + 1, s_z)
                if not last:
                    v_rest(b + 1, 7)

            s_lnx, s_lnn, s_lnz, s_topi, s_topf, s_ea1 = s_own

            dve.wait_ge(s_const, 16)
            ln_x_stats(0)
            ln_x(0, None)
            for n in range(3):
                for c in range(KC):
                    dve.wait_ge(s_whead, 2 * n + c + 1)
                    if n == 0:
                        dve.scalar_tensor_tensor(wl[:, n, c, :], w_raw[:, n, c, :], 1.0 / DH,
                                                 wh[:, n, c, :].bitcast(F32),
                                                 ALU.mult, ALU.subtract).then_inc(s_wrest, 1)
                    else:
                        dve.tensor_tensor(wl[:, n, c, :], w_raw[:, n, c, :], wh[:, n, c, :].bitcast(F32),
                                          ALU.subtract).then_inc(s_wrest, 1)
            xt_rest(0)
            for n in (0, 2):
                times_cos(n, 0)
                k_products(n)
            for m in range(2 * NI):
                v_rest(0, m)
            batch(0, first=True)
            with dve.Fori(1, B - 1) as b:
                batch(b)
            batch(B - 1, last=True)
            dve.wait_ge(s_obread, obn(B))
            choose(B - 1)
            gate(B - 1)

            rc = [0]

            def own(ins):
                rc[0] += 1
                ins.then_inc(s_dve, 1)
                dve.wait_ge(s_dve, rc[0])

            flat = lambda a: a[:, :, :].rearrange("p a b -> p (a b)")
            dve.wait_ge(s_count, 1)
            own(dve.tensor_copy(tot[:, :, :].rearrange("p e t -> p t e"),
                                SB[1][:, 0:NT * E].rearrange("p (t e) -> p t e", e=E)))
            own(dve.tensor_tensor_scan(flat(cum), ones_f[:, :], flat(tot), 0.0, ALU.mult, ALU.add))
            own(dve.tensor_copy(cnt[:, :], cum[:, :, NT - 1]))
            own(dve.tensor_tensor(adj2[:, 1:E], cnt[:, 1:E], cnt[:, 0:E - 1], ALU.subtract))
            own(dve.tensor_copy(adj2[:, 0:1], cnt[:, 0:1]))
            own(dve.tensor_scalar(cnt_i[:, :], adj2[:, :], float(P - 1), None, ALU.add))
            own(dve.tensor_scalar(tiles_i[:, :], cnt_i[:, :], 7, None, ALU.logical_shift_right))
            own(dve.tensor_copy(tiles_f[:, :], tiles_i[:, :]))
            own(dve.tensor_tensor_scan(tiles_cum[:, :], ones_f[:, 0:E], tiles_f[:, :], 0.0, ALU.mult, ALU.add))
            own(dve.tensor_tensor(adj[:, :], tiles_cum[:, :], tiles_f[:, :], ALU.subtract))
            own(dve.scalar_tensor_tensor(adj[:, :], adj[:, :], float(P), cnt[:, :], ALU.mult, ALU.subtract))
            own(dve.tensor_tensor(adj[:, :], adj[:, :], adj2[:, :], ALU.add))
            own(dve.tensor_tensor(flat(cum), flat(cum), flat(tot), ALU.subtract))
            own(dve.tensor_tensor(cum[:, :, :], cum[:, :, :],
                                  adj[:, :].rearrange("p (e o) -> p e o", o=1).broadcast_to([P, E, NT]), ALU.add))
            own(dve.tensor_tensor(pos[:, :, :], SB[0][:, 0:NT * E].rearrange("p (t e) -> p t e", e=E),
                                  cum[:, :, :].rearrange("p e t -> p t e"), ALU.add))
            own(dve.tensor_tensor(pos[:, :, :], pos[:, :, :], onehot[:, :, :], ALU.mult))
            own(dve.tensor_reduce(slot[:, :], pos[:, :, :], AX.X, ALU.add))
            own(dve.tensor_copy(slot_i[:, :], slot[:, :]))
            own(dve.tensor_scalar(hi_i[:, :], slot_i[:, :], 7, None, ALU.logical_shift_right))
            own(dve.tensor_scalar(lo_i[:, :], slot_i[:, :], P - 1, None, ALU.bitwise_and))
            own(dve.tensor_copy(slot_hi[:, :], hi_i[:, :]))
            own(dve.tensor_copy(slot_lo[:, :], lo_i[:, :]))
            wide = lambda a, n: a.rearrange("p (t o) -> p t o", o=1).broadcast_to([P, 4, n])
            count = lambda n: cst[:, C_IOTA:C_IOTA + n].rearrange("p (o n) -> p o n", o=1).broadcast_to([P, 4, n])
            for g in range(NT // 4):
                ts, k = slice(4 * g, 4 * g + 4), slice(g % 2 * 4, g % 2 * 4 + 4)
                if g >= 2:
                    dve.wait_ge(s_routeb, g - 1)
                dve.tensor_tensor(hot_hi[:, k, :], count(NS), wide(slot_hi[:, ts], NS),
                                  ALU.is_equal).then_inc(s_hhi, 1)
                dve.tensor_tensor(hot_lo[:, k, :], count(P), wide(slot_lo[:, ts], P), ALU.is_equal)
                dve.wait_ge(s_hhi, g + 1)
                dve.tensor_tensor(hot_hi[:, k, :], hot_hi[:, k, :],
                                  wide(cst[:, C_TOK + 4 * g:C_TOK + 4 * g + 4], NS), ALU.mult).then_inc(s_route, 1)
            own(dve.tensor_tensor(below[:, :, :],
                                  tiles_cum[:, :].rearrange("p (o e) -> p o e", o=1).broadcast_to([P, NS, E]),
                                  cst[:, C_IOTA:C_IOTA + NS].rearrange("p (j o) -> p j o", o=1).broadcast_to([P, NS, E]),
                                  ALU.is_le))
            own(dve.tensor_reduce(below_n[:, :], below[:, :, :], AX.X, ALU.add))
            dve.tensor_scalar(tile_exp[:, :], below_n[:, :], float(E - 1), None, ALU.min).then_inc(s_texp, 1)
            dve.wait_ge(s_routeb, NT // 4)
            dve.tensor_scalar(slot_tok[:, :], PT[0][:, 0:NS], float(B * T), None, ALU.add).then_inc(s_idx, 1)

            dve.wait_ge(s_texp, 1)
            dve.wait_ge(s_fw, FW)

            def affine(j, k, e):
                dve.wait_ge(s_zt, j + 1)
                for c in range(KC):
                    ins = dve.tensor_scalar(ht[:, k % 2, c, :], FZ[:, c * P:(c + 1) * P],
                                            g_col[:, bass.ds(e, 1), c:c + 1].rearrange("p a b -> p (a b)"),
                                            b_col[:, bass.ds(e, 1), c:c + 1].rearrange("p a b -> p (a b)"),
                                            ALU.mult, ALU.add)
                ins.then_inc(s_ht, 1)

            def h1_out(j, k):
                dve.wait_ge(s_h1, 2 * j + 2)
                dve.tensor_copy(h1[:, k % 2, 512:1024], FH[1][:, :]).then_inc(s_h1d, 1)

            def h1t_out(j, k, e):
                dve.wait_ge(s_hT, 2 * j + 2)
                for c in range(4, 8):
                    ins = dve.tensor_scalar(h1t[:, k % 2, c, :], FT[1][:, (c - 4) * P:(c - 3) * P],
                                            b1_col[:, bass.ds(e, 1), c:c + 1].rearrange("p a b -> p (a b)"), 0.0,
                                            ALU.add, ALU.max)
                ins.then_inc(s_hTd, 1)

            def combine(j, k, e, again):
                dve.wait_ge(s_y, j + 1)
                dve.tensor_tensor(yb[:, k % 2, :], FY[k % 2][:, 0:D],
                                  b2_all[:, bass.ds(e, 1), :].rearrange("p o d -> p (o d)"),
                                  ALU.add).then_inc(s_yb, 1)
                if again is not None:
                    dve.wait_ge(s_sca[k % 3], 16 * again)
                dve.wait_ge(s_yb, j + 1)
                dve.scalar_tensor_tensor(row_out[:, k % 3, :], yb[:, k % 2, :], row_in[:, k % 6, 2 * D:2 * D + 1],
                                         row_in[:, k % 6, D:2 * D], ALU.mult, ALU.add).then_inc(s_comb, 1)

            def expert(j):
                return dve.value_load(tile_exp[0:1, bass.ds(j, 1)], min_val=0, max_val=E - 1)

            e = expert(0)
            affine(0, 0, e)
            h1_out(0, 0)
            h1t_out(0, 0, e)
            affine(1, 1, expert(1))

            def step(j, k, again, left=3):
                if left > 2:
                    e2 = expert(j + 2)
                if left > 1:
                    h1_out(j + 1, k + 1)
                if left > 2:
                    affine(j + 2, k + 2, e2)
                combine(j, k, expert(j), again)
                if left > 1:
                    h1t_out(j + 1, k + 1, expert(j + 1))

            for j in range(3):
                step(j, j, None)
            with dve.Fori(0, NS // 6 - 1) as it:
                for k in range(6):
                    step(6 * it + 3 + k, 3 + k, 2 * it + 1 + k // 3)
            for j in range(NS - 6, NS):
                step(j, j, j // 3, NS - j)


_INS = ["x", "w_q", "w_k", "w_v", "w_o", "cent_t", "ln_g", "ln_b", "w1_t", "b1", "w2_t", "b2", "consts"]


def constants():
    import numpy as np
    f = np.float32
    c = np.zeros((P, C_END), f)
    half = DH // 2
    freqs = np.power(f(10000.0), -(np.arange(half, dtype=f) / f(half))).astype(f)
    rad = (np.arange(T, dtype=f)[:, None] * freqs[None, :]).astype(f)
    cos, sin = np.cos(rad).astype(f), np.sin(rad).astype(f)
    d = np.arange(P) % half
    c[:, C_COS:C_COS + T] = cos.T[d]
    c[:, C_SIN:C_SIN + T] = np.where(np.arange(P)[:, None] < half, -sin.T[d], sin.T[d])
    c[:, C_IOTA:C_IOTA + P] = np.arange(P)[None, :]
    c[:, C_TOK:C_TOK + NT] = np.arange(P)[:, None] + P * np.arange(NT)[None, :] - B * T
    c[:, C_ID:C_ID + P] = np.eye(P)
    p, n = np.arange(P)[:, None], np.arange(P)[None, :]
    c[:, C_MASK:C_MASK + P] = np.where(n > p, f(-1e30), f(0.0))
    c[:, C_LT:C_LT + P] = (p < n)
    return c


def kernel(**inputs):
    import numpy as np
    import concourse.bacc as bacc
    from concourse.bass_utils import run_bass_kernel_spmd

    g = {k[3:]: np.asarray(a) for k, a in inputs.items()}
    arrays = {
        "x": g["attn_x"], "w_q": g["attn_w_aq"].reshape(D, H * DH), "w_k": g["attn_w_ak"].reshape(D, H * DH),
        "w_v": g["attn_w_av"].reshape(D, H * DH), "w_o": g["attn_w_ao"].reshape(H * DH, D),
        "cent_t": g["ffn_centroids"].T, "ln_g": g["ffn_ln_g"], "ln_b": g["ffn_ln_b"],
        "w1_t": g["ffn_w1"].transpose(0, 2, 1), "b1": g["ffn_b1"],
        "w2_t": g["ffn_w2"].transpose(0, 2, 1), "b2": g["ffn_b2"], "consts": constants(),
    }
    arrays = {k: np.ascontiguousarray(a) for k, a in arrays.items()}
    nc = bacc.Bacc("TRN2", target_bir_lowering=False, num_devices=1)
    ins = [nc.dram_tensor(k, arrays[k].shape, F32, kind="ExternalInput").ap() for k in _INS]
    out = nc.dram_tensor("out", (B, T, D), F32, kind="ExternalOutput").ap()
    tok_rows = nc.dram_tensor("tok_rows", (B * T + 1, ROW), F32, kind="Internal").ap()
    build(nc, *ins, out, tok_rows)
    r = run_bass_kernel_spmd(nc, [arrays], core_ids=[0])
    return r.results[0]["out"]
```

```python
from contextlib import ExitStack

import concourse.bass as bass
from concourse import mybir

F32 = mybir.dt.float32
F32R = mybir.dt.float32r
BF16 = mybir.dt.bfloat16
I32 = mybir.dt.int32
U32 = mybir.dt.uint32
ACT = mybir.ActivationFunctionType
ALU = mybir.AluOpType
AX = mybir.AxisListType

P = 128
EPS = 1e-5
B, T, D = 8, 512, 256
H, DH = 8, 128
E, F = 8, 1024
NI = T // P
KC = D // P
FC = F // P
NT = B * NI
NS = NT + E - 1
ROW = 2 * D + 4
POFF = [0, 128, 384, 768]
TOFF = [0, 512, 896, 1152]
CAUSAL = NI * (NI + 1) // 2 * P
CHUNK = [(0, 512), (512, 384), (896, 384)]

C_COS, C_SIN = 0, T
C_IOTA = 2 * T
C_TOK = C_IOTA + P
C_PART = C_TOK + NT
C_ID = C_PART + 1
C_MASK = C_ID + P
C_LT = C_MASK + P
C_END = C_LT + P


def build(nc, x, w_q, w_k, w_v, w_o, cent_t, ln_g, ln_b, w1_t, b1, w2_t, b2, consts, out, tok_rows):
    ctx = ExitStack()
    with ctx:
        sem = lambda n: ctx.enter_context(nc.semaphore(n))

        base = (nc.sbuf_base + 63) // 64 * 64
        place = [base]
        size = {F32: 4, F32R: 4, BF16: 2, I32: 4, U32: 4}

        def sb(name, shape, dt):
            n = size[dt]
            for s in shape[1:]:
                n *= s
            t = nc.alloc_sbuf_tensor_at(name, shape, dt, offset=place[0])
            place[0] += (n + 31) // 32 * 32
            assert place[0] <= nc.sbuf_usable_end, (name, place[0])
            return t

        onehot = sb("onehot", [P, NT, E], BF16)
        cst = sb("cst", [P, C_END], F32)
        ident = cst[:, C_ID:C_ID + P]
        ident_b = sb("ident_b", [P, P], BF16)
        mask_b = sb("mask_b", [P, P], BF16)
        lower_b = sb("lower_b", [P, P], BF16)
        ones_b = sb("ones_b", [P, P], BF16)
        cent = sb("cent", [P, KC, E], F32)
        slot_hi = sb("slot_hi", [P, NT], F32)
        slot_lo = sb("slot_lo", [P, NT], F32)
        slot_tok = sb("slot_tok", [P, NS], U32)
        tok_now = sb("tok_now", [P, 6], U32)
        tile_exp = sb("tile_exp", [P, NS], I32)
        ones_f = sb("ones_f", [P, E * NT], F32)
        common_end = place[0]

        xa = sb("xa", [P, NI, D], F32)
        xh = sb("xh", [P, NI, D], F32)
        xth = sb("xth", [P, KC, T], F32R)
        xtl = sb("xtl", [P, KC, T], F32R)
        wh = sb("wh", [P, 3, KC, H * DH], F32R)
        wl = sb("wl", [P, 3, KC, H * DH], F32R)
        w_raw_at = place[0]
        qkh = sb("qkh", [P, 4, 2, T], F32R)
        qkl = sb("qkl", [P, 4, 2, T], F32R)
        rope_c = sb("rope_c", [P, 2, T], F32)
        rope_s = sb("rope_s", [P, 2, T], F32)
        w_raw = nc.alloc_sbuf_tensor_at("w_raw", [P, 3, KC, H * DH], F32, offset=w_raw_at)
        prob = sb("prob", [P, 2, CAUSAL], F32)
        wo = sb("wo", [P, H, D], F32)
        vh = sb("vh", [P, NI, H * DH], F32R)
        vl = sb("vl", [P, NI, H * DH], F32R)
        xr = sb("xr", [P, NI, D], F32)
        routing_at = place[0]
        pth = sb("pth", [P, CAUSAL], F32R)
        ptl = sb("ptl", [P, CAUSAL], F32R)
        ot = sb("ot", [P, H, T], F32)
        routing_end = place[0]
        x1 = sb("x1", [P, NI, D], F32)
        xn = sb("xn", [P, NI, D], F32)
        xnt = sb("xnt", [P, KC, T], F32)
        gates = sb("gates", [P, NI, ROW - 2 * D], F32)
        negmax = sb("negmax", [P, 2, NI], F32)
        denom = sb("denom", [P, 2, NI], F32)
        rdenom = sb("rdenom", [P, 2, NI], F32)
        stats = [sb(f"stats{k}", [P, NI, 6], F32) for k in range(3)]
        mv = [sb(f"mv{k}", [P, NI, 2], F32) for k in range(3)]
        veps = [sb(f"veps{k}", [P, NI], F32) for k in range(3)]
        rstd = [sb(f"rstd{k}", [P, NI], F32) for k in range(3)]
        zero_row = sb("zero_row", [ROW // 6, 6], F32)
        mhalf = sb("mhalf", [P, NI], F32)
        aff = sb("aff", [P, NI, E], F32)
        top = sb("top", [P, NI, 8], F32)
        topi = sb("topi", [P, NI, 8], U32)
        topf = sb("topf", [P, NI], F32)
        ealpha = sb("ealpha", [P, NI], F32)
        ealpha1 = sb("ealpha1", [P, NI], F32)
        attn_end = place[0]

        place[0] = common_end
        b2_all = sb("b2_all", [P, E, D], F32)
        b1_col = sb("b1_col", [P, E, FC], F32)
        g_col = sb("g_col", [P, E, KC], F32)
        b_col = sb("b_col", [P, E, KC], F32)
        w2s = sb("w2s", [P, E, 2, FC * D], F32R)
        w1r = sb("w1r", [P, 3, KC * F], F32)
        w1r_end = place[0]
        row_in = sb("row_in", [P, 6, ROW], F32)
        row_out = sb("row_out", [P, 3, D], F32)
        ht = sb("ht", [P, 2, KC, P], F32)
        hid = sb("hid", [P, FC, P], F32)
        hidh = sb("hidh", [P, 2, FC, P], F32R)
        hidl = sb("hidl", [P, 2, FC, P], F32R)
        ffn_end = place[0]
        place[0] = max(routing_at, w1r_end)
        tot = sb("tot", [P, E, NT], F32)
        cum = sb("cum", [P, E, NT], F32)
        cnt = sb("cnt", [P, E], F32)
        cnt_i = sb("cnt_i", [P, E], I32)
        tiles_i = sb("tiles_i", [P, E], I32)
        tiles_f = sb("tiles_f", [P, E], F32)
        tiles_cum = sb("tiles_cum", [P, E], F32)
        adj = sb("adj", [P, E], F32)
        adj2 = sb("adj2", [P, E], F32)
        pos = sb("pos", [P, NT, E], F32)
        slot = sb("slot", [P, NT], F32)
        slot_i = sb("slot_i", [P, NT], I32)
        hi_i = sb("hi_i", [P, NT], I32)
        lo_i = sb("lo_i", [P, NT], I32)
        below = sb("below", [P, NS, E], F32)
        below_n = sb("below_n", [P, NS], F32)
        hot_lo = sb("hot_lo", [P, 16, P], BF16)
        hot_tile = sb("hot_tile", [P, 8, NS], F32)
        hot_tok = sb("hot_tok", [P, 16, 2, NS], BF16)
        tok_hi = sb("tok_hi", [P, NS], F32)

        assert place[0] <= routing_end
        bank = [ctx.enter_context(nc.psum_tensor(f"bank{n}", [P, 512], F32)) for n in range(8)]
        PP = bank[0:2]
        SB = bank[2:4]
        PT = bank[4:7]
        OB = bank[7]
        FZ, FH, FY = bank[0], bank[1:5], bank[5:7]

        s_const = sem("const_loaded")
        s_wraw = [sem(f"w_{n}_raw_loaded") for n in "qkv"]
        s_wsmall = sem("w_small_loaded")
        s_whead = sem("w_head_made")
        s_wrest = [sem(f"w_{n}_rest_made") for n in "qkv"]
        s_cb = sem("bf16_consts_made")
        s_xa = sem("xa_loaded")
        s_xr = sem("xr_loaded")
        s_xmean = sem("x_stats_made")
        s_xrstd = sem("x_rstd_made")
        s_xveps = sem("x_veps_made")
        s_xh = sem("xh_made")
        s_ppdone = sem("pp_written")
        s_ppread = sem("pp_read")
        s_xth = sem("xt_head_made")
        s_vh = sem("v_head_made")
        s_swap = sem("halves_swapped")
        s_qsin = sem("q_times_sin_made")
        s_kprod = sem("k_products_made")
        s_rope = sem("rope_summed")
        s_qkh = sem("qk_head_made")
        s_qkl = sem("qk_rest_made")
        s_score = sem("scores_written")
        s_max = sem("max_made")
        s_exp = sem("exp_made")
        s_rden = sem("rdenom_made")
        s_pscaled = sem("probs_scaled")
        s_ptdone = sem("pt_written")
        s_pth = sem("pt_head_made")
        s_ptl = sem("pt_rest_made")
        s_obdone = sem("ob_written")
        s_obread = sem("ob_read")
        s_dve = sem("dve_step")
        s_own = [sem(n) for n in ("x_bn_made", "x1_bn_made", "xn_bn_made", "top_index_made", "top_float_made",
                                  "exp_plus_one_made")]
        s_nstat = sem("x1_stats_made")
        s_nveps = sem("x1_veps_made")
        s_nrstd = sem("x1_rstd_made")
        s_xn = sem("xn_made")
        s_zstat = sem("xn_stats_made")
        s_zveps = sem("xn_veps_made")
        s_zrstd = sem("xn_rstd_made")
        s_skip = sem("skip_made")
        s_z = sem("z_made")
        s_top = sem("top_made")
        s_ea = sem("exp_neg_top_made")
        s_gate = sem("gate_made")
        s_rows = sem("rows_stored")
        s_zrow = sem("zero_row_made")
        s_pool = sem("pool_constants_made")

        s_hot = sem("onehots_made")
        s_count = sem("counts_written")
        s_hhi = sem("slot_tile_hot_made")
        s_route = sem("slot_hot_made")
        s_routeb = sem("slot_hot_used")
        s_idx = sem("slot_tok_made")
        s_texp = sem("tile_exp_made")

        s_fsmall = sem("ffn_vectors_loaded")
        s_w2 = [sem(f"w2_{e}_loaded") for e in range(E)]
        s_w2h = sem("w2_head_made")
        s_w2l = [sem("w2_rest_made_by_pool"), sem("w2_rest_made_by_dve")]
        s_w1 = [sem(f"w1_loaded{k}") for k in range(3)]
        s_gat = [sem(f"row_gathered{k}") for k in range(6)]
        s_sca = [sem(f"row_scattered{k}") for k in range(3)]
        s_passed = sem("wait_passed")
        s_now = sem("tok_now_made")
        s_zt = sem("zt_written")
        s_ht = sem("ht_made")
        s_h1 = sem("h1_written")
        s_hid = sem("hidden_made")
        s_hidh = sem("hidden_head_made")
        s_hidl = sem("hidden_rest_made")
        s_y = sem("y_written")
        s_yb = sem("y_biased")
        s_comb = sem("row_combined")

        PPN = lambda b: 14 + 30 * b
        UN = lambda b: 4 + 16 * b
        obn = lambda b: 11 * b

        def unit_at(b, h):
            k = h if h < 7 else h - 1
            return UN(b) + 2 * k, PPN(b) + 2 * h, (k + 2) % 4

        def has_units(h, last):
            return h < 6 or (h > 6 and not last)

        def split_k(h, last):
            return 0 < h < 7 or (h == 8 and not last)

        ROWS = lambda b: 16 + 48 * b

        x_v = x.rearrange("b (i p) d -> b p i d", p=P)
        rows_v = tok_rows[0:B * T, :].rearrange("(b i p) r -> b p i r", p=P, i=NI)
        out_v = out.rearrange("b t d -> (b t) d")

        block = ctx.enter_context(nc.Block())

        def passed(eng):
            eng.sem_inc(s_passed, 1)

        def w_rest(eng, n, chunks=range(KC)):
            for c in chunks:
                eng.wait_ge(s_whead, 2 * n + c + 1)
                eng.tensor_tensor(wl[:, n, c, :], w_raw[:, n, c, :], wh[:, n, c, :].bitcast(F32),
                                  ALU.subtract).then_inc(s_wrest[n], 1)

        def w2_rest(eng, which, e):
            eng.wait_ge(s_w2h, e + 1)
            eng.tensor_tensor(w2s[:, e, 1, :], w2s[:, e, 1, :].bitcast(F32), w2s[:, e, 0, :].bitcast(F32),
                              ALU.subtract).then_inc(s_w2l[which], 1)

        @block.sync
        def _(sp):
            sp.dma_start(xa[:, :, :], x_v[0]).then_inc(s_xa, 16)
            for n, w in ((0, w_q), (1, w_k), (2, w_v)):
                sp.dma_start(w_raw[:, n, :, :], w.rearrange("(c p) n -> p c n", p=P)).then_inc(s_wraw[n], 16)
                if n == 0:
                    sp.dma_start(cst[:, :], consts).then_inc(s_const, 16)
            sp.dma_start(wo[:, :, :], w_o.rearrange("(h p) n -> p h n", p=P)).then_inc(s_wsmall, 16)
            sp.dma_start(cent[:, :, :], cent_t.rearrange("(c p) e -> p c e", p=P)).then_inc(s_wsmall, 16)
            sp.dma_start(xr[:, :, :], x_v[0]).then_inc(s_xr, 16)
            sp.wait_ge(s_xh, 1)
            sp.dma_start(xa[:, :, :], x_v[1]).then_inc(s_xa, 16)
            sp.wait_ge(s_zrow, 1)
            sp.dma_start(tok_rows[B * T:B * T + 1, :].rearrange("o (p c) -> (o p) c", c=6),
                         zero_row[:, :]).then_inc(s_rows, 16)
            sp.wait_ge(s_rows, 16)

            def store_rows(b):
                place_b = rows_v[bass.ds(b, 1)].rearrange("o p i r -> (o p) i r")
                sp.wait_ge(s_skip, b + 1)
                passed(sp)
                sp.dma_start(place_b[:, :, D:2 * D], x1[:, :, :]).then_inc(s_rows, 16)
                sp.wait_ge(s_z, b + 1)
                passed(sp)
                sp.dma_start(place_b[:, :, 0:D], xn[:, :, :]).then_inc(s_rows, 16)
                sp.wait_ge(s_gate, b + 1)
                passed(sp)
                sp.dma_start(place_b[:, :, 2 * D:ROW], gates[:, :, :]).then_inc(s_rows, 16)

            def load_xr(b):
                sp.wait_ge(s_ppread, PPN(b) - 6)
                sp.dma_start(xr[:, :, :], x_v[bass.ds(b, 1)].rearrange("o p i d -> (o p) i d")).then_inc(s_xr, 16)

            def load_xa(b):
                sp.wait_ge(s_xh, b)
                sp.dma_start(xa[:, :, :], x_v[bass.ds(b, 1)].rearrange("o p i d -> (o p) i d")).then_inc(s_xa, 16)

            with sp.Fori(1, B - 1) as b:
                load_xa(b + 1)
                load_xr(b)
                store_rows(b - 1)
            load_xr(B - 1)
            store_rows(B - 2)

            def load_w2(e):
                sp.dma_start(w2s[:, e, 1, :].bitcast(F32).rearrange("p (c d) -> p c d", c=FC),
                             w2_t[e].rearrange("(c p) d -> p c d", p=P)).then_inc(s_w2[e], 16)

            sp.wait_ge(s_ppdone, PPN(B - 1) + 12)
            for t, src in ((g_col, ln_g), (b_col, ln_b)):
                sp.dma_start(t[:, :, :], src.rearrange("e (c p) -> p e c", p=P),
                             allow_slow_non_contiguous=True).then_inc(s_fsmall, 16)
            sp.dma_start(b1_col[:, :, :], b1.rearrange("e (c p) -> p e c", p=P),
                         allow_slow_non_contiguous=True).then_inc(s_fsmall, 16)
            sp.dma_start(b2_all[:, :, :].rearrange("p e d -> p (e d)"),
                         b2.rearrange("e d -> (e d)").rearrange("(o n) -> o n", o=1).broadcast_to([P, E * D])
                         ).then_inc(s_fsmall, 16)
            for e in range(3):
                load_w2(e)
            sp.wait_ge(s_score, 32 * B)
            load_w2(3)
            sp.wait_ge(s_ptdone, 24 * B)
            load_w2(4)
            sp.wait_ge(s_ppread, PPN(B - 1) + 16)
            load_w2(5)
            load_w2(6)
            load_w2(7)
            store_rows(B - 1)

            sp.wait_ge(s_texp, 1)

            def load_w1(j, k, wait):
                e = sp.value_load(tile_exp[0:1, bass.ds(j, 1)], min_val=0, max_val=E - 1)
                if wait is not None:
                    sp.wait_ge(s_h1, wait)
                    passed(sp)
                sp.dma_start(w1r[:, k % 3, :].rearrange("p (c f) -> p c f", c=KC),
                             w1_t[bass.ds(e, 1)].rearrange("o (c p) f -> (o p) c f", p=P)).then_inc(s_w1[k % 3], 16)

            for j in range(3):
                load_w1(j, j, None)
            with sp.Fori(1, NS // 3) as it:
                for k in range(3):
                    load_w1(3 * it + k, k, 6 * it + 2 * k - 4)

        @block.gpsimd
        def _(pool):
            pool.memset(mhalf[:, :], -0.5).then_inc(s_pool, 1)
            pool.memset(ones_b[:, :], 1.0).then_inc(s_cb, 1)
            pool.memset(ones_f[:, :], 1.0).then_inc(s_cb, 1)
            pool.memset(zero_row[:, :], 0.0).then_inc(s_zrow, 1)
            pool.memset(gates[:, :, 1:ROW - 2 * D], 0.0).then_inc(s_pool, 1)
            pool.wait_ge(s_pool, 2)

            def power(k, stat, made, done, n):
                pool.wait_ge(stat, n + 1)
                passed(pool)
                pool.tensor_scalar(veps[k][:, :], mv[k][:, :, 1], EPS, None, ALU.add).then_inc(made, 1)
                pool.wait_ge(made, n + 1)
                pool.tensor_tensor(rstd[k][:, :], veps[k][:, :], mhalf[:, :], ALU.pow).then_inc(done, 1)

            def rope_sum(n, g, kind):
                if kind == 0:
                    pool.wait_ge(s_swap, n + 1)
                    pool.tensor_tensor(rope_s[:, 0, :], rope_s[:, 0, :], cst[:, C_SIN:C_SIN + T],
                                       ALU.mult).then_inc(s_qsin, 2)
                    pool.wait_ge(s_qsin, n + 2)
                    pool.wait_ge(s_ppread, g + 1)
                else:
                    pool.wait_ge(s_kprod, n + 2)
                pool.tensor_tensor(rope_c[:, kind, :], rope_c[:, kind, :], rope_s[:, kind, :],
                                   ALU.add).then_inc(s_rope, 1)

            def qk_rest(n, par, kind):
                pool.wait_ge(s_qkh, n + kind + 1)
                pool.tensor_tensor(qkl[:, par, kind, :], rope_c[:, kind, :], qkh[:, par, kind, :].bitcast(F32),
                                   ALU.subtract).then_inc(s_qkl, 1)

            def skip(b):
                pool.wait_ge(s_xn, b + 1)
                pool.tensor_tensor(x1[:, :, :], x1[:, :, :], xn[:, :, :], ALU.add).then_inc(s_skip, 1)

            def batch(b, last=False):
                for h in range(H + 1):
                    n, g, par = unit_at(b, h)
                    if split_k(h, last):
                        qk_rest(n - 2, (par - 1) % 4, 1)
                    if has_units(h, last):
                        rope_sum(n, g, 0)
                        qk_rest(n, par, 0)
                        rope_sum(n, g, 1)
                    if h == 2 and not last:
                        power(0, s_xmean, s_xveps, s_xrstd, b + 1)
                if last:
                    w2_rest(pool, 0, 0)
                    w2_rest(pool, 0, 1)
                else:
                    qk_rest(UN(b) + 14, 1, 1)
                power(1, s_nstat, s_nveps, s_nrstd, b)
                skip(b)
                power(2, s_zstat, s_zveps, s_zrstd, b)
                if last:
                    for e in range(2, 5):
                        w2_rest(pool, 0, e)

            power(0, s_xmean, s_xveps, s_xrstd, 0)
            w_rest(pool, 1, [0])
            for head in range(2):
                for kind in range(2):
                    rope_sum(2 * head, 2 + 2 * head, kind)
                    qk_rest(2 * head, head, kind)
            batch(0)
            with pool.Fori(1, B - 1) as b:
                batch(b)
            batch(B - 1, last=True)

            pool.wait_ge(s_rows, ROWS(B))
            pool.wait_ge(s_idx, 1)

            def gather(j, k, again=None):
                if again is not None:
                    pool.wait_ge(s_sca[k % 3], 16 * again)
                pool.tensor_copy(tok_now[:, k % 6:k % 6 + 1], slot_tok[:, bass.ds(j, 1)]).then_inc(s_now, 1)
                pool.wait_ge(s_now, j + 1)
                passed(pool)
                pool.indirect_dma_start(row_in[:, k % 6, :], None, tok_rows,
                                        bass.IndirectOffsetOnAxis(ap=tok_now[:, k % 6:k % 6 + 1], axis=0)
                                        ).then_inc(s_gat[k % 6], 16)

            def scatter(j, k):
                pool.wait_ge(s_comb, j + 1)
                passed(pool)
                pool.indirect_dma_start(out_v, bass.IndirectOffsetOnAxis(ap=tok_now[:, k % 6:k % 6 + 1], axis=0),
                                        row_out[:, k % 3, :], None, bounds_check=B * T - 1, oob_is_err=False
                                        ).then_inc(s_sca[k % 3], 16)

            for j in range(5):
                gather(j, j)
            for j in range(6):
                scatter(j, j)
                gather(j + 5, j + 5, None if j == 0 else (j - 1) // 3 + 1)
            with pool.Fori(1, NS // 6 - 1) as it:
                for k in range(6):
                    scatter(6 * it + k, k)
                    gather(6 * it + k + 5, k + 5, 2 * it + (k - 1) // 3 + 1)
            for j in range(NS // 6 * 6 - 6, NS):
                scatter(j, j)
                if j + 5 < NS:
                    gather(j + 5, j + 5, (j - 1) // 3 + 1)
            for k in range(3):
                pool.wait_ge(s_sca[k], 16 * (NS // 3))

        @block.scalar
        def _(act):
            def w_head(n):
                act.wait_ge(s_wraw[n], 16)
                for c in range(KC):
                    act.activation(wh[:, n, c, :], w_raw[:, n, c, :], ACT.Copy,
                                   scale=1.0 / DH if n == 0 else 1.0).then_inc(s_whead, 1)

            def xt_head(g):
                for c in range(KC):
                    act.wait_ge(s_ppdone, g + c + 1)
                    act.activation(xth[:, c, :], PP[c][:, :], ACT.Copy).then_inc(s_xth, 1)

            def v_head(g, m):
                act.wait_ge(s_ppdone, g + 1)
                act.activation(vh[:, m // 2, (m % 2) * 512:(m % 2) * 512 + 512], PP[m % 2][:, :],
                               ACT.Copy).then_inc(s_vh, 1)

            def swap(n, g, kind):
                act.wait_ge(s_ppdone, g + kind + 1)
                if not (isinstance(n, int) and n + kind < 2):
                    act.wait_ge(s_rope, n + kind - 1)
                act.activation(rope_s[0:64, kind, :], PP[kind][64:128, :], ACT.Copy)
                act.activation(rope_s[64:128, kind, :], PP[kind][0:64, :], ACT.Copy).then_inc(s_swap, 1)

            def qk_head(n, par, kind):
                act.wait_ge(s_rope, n + kind + 1)
                act.activation(qkh[:, par, kind, :], rope_c[:, kind, :], ACT.Copy).then_inc(s_qkh, 1)

            def exps(b, h, i):
                n = 32 * b + 4 * h + i
                act.wait_ge(s_max, n + 1)
                act.activation(prob[:, h % 2, POFF[i]:POFF[i] + (i + 1) * P], SB[i % 2][:, 0:(i + 1) * P], ACT.Exp,
                               bias=negmax[:, h % 2, i:i + 1], scale=1.0,
                               accum_out=denom[:, h % 2, i:i + 1]).then_inc(s_exp, 1)

            def pt_head(b, h, c):
                act.wait_ge(s_ptdone, 24 * b + 3 * h + c + 1)
                lo, w = CHUNK[c]
                act.activation(pth[:, lo:lo + w], PT[c][:, 0:w], ACT.Copy).then_inc(s_pth, 1)

            def o_out(b, h):
                act.wait_ge(s_obdone, obn(b) + h + 1)
                act.activation(ot[:, h, :], OB[:, :], ACT.Copy).then_inc(s_obread, 1)

            def xn_out(n, c):
                act.wait_ge(s_obdone, n + 1)
                act.activation(xnt[:, c, :], OB[:, :], ACT.Copy).then_inc(s_obread, 1)

            def aff_out(n):
                act.wait_ge(s_obdone, n + 1)
                act.activation(aff[:, :, :], OB[:, 0:NI * E].rearrange("p (i e) -> p i e", i=NI),
                               ACT.Copy).then_inc(s_obread, 1)

            def gate_exp(b):
                act.wait_ge(s_top, b + 1)
                act.activation(ealpha[:, :], top[:, :, 0], ACT.Exp, scale=-1.0).then_inc(s_ea, 1)

            def w2_head(e):
                act.wait_ge(s_w2[e], 16)
                act.activation(w2s[:, e, 0, :], w2s[:, e, 1, :].bitcast(F32), ACT.Copy).then_inc(s_w2h, 1)

            def batch(b, last=False):
                ob = obn(b)
                for h in range(H + 1):
                    n, g, par = unit_at(b, h)
                    unit = has_units(h, last)
                    if h < H:
                        exps(b, h, 0)
                    if h >= 2:
                        o_out(b, h - 2)
                    if h < H:
                        exps(b, h, 1)
                    if split_k(h, last):
                        qk_head(n - 2, (par - 1) % 4, 1)
                    if unit:
                        swap(n, g, 0)
                    if h == 6 and not last:
                        xt_head(g)
                    if h >= 1:
                        pt_head(b, h - 1, 0)
                    if h < H:
                        exps(b, h, 2)
                    if h >= 1:
                        pt_head(b, h - 1, 1)
                        pt_head(b, h - 1, 2)
                    if unit:
                        swap(n, g, 1)
                    if unit and h > 0:
                        qk_head(n, par, 0)
                    if h < H:
                        exps(b, h, 3)
                    if h == 0:
                        qk_head(n, par, 0)
                    if h == 3 and not (isinstance(b, int) and b == 0):
                        gate_exp(b - 1)
                o_out(b, H - 1)
                if last:
                    for e in range(3):
                        w2_head(e)
                    xn_out(ob + 8, 0)
                    xn_out(ob + 9, 1)
                    aff_out(ob + 10)
                else:
                    for m in range(2 * NI):
                        v_head(PPN(b) + 18 + m + (0 if m < 2 else NI), m)
                        if m == 1:
                            qk_head(UN(b) + 14, 1, 1)
                        if m == 4:
                            xn_out(ob + 8, 0)
                        if m == 5:
                            xn_out(ob + 9, 1)
                        if m == 6:
                            aff_out(ob + 10)

            w_head(0)
            act.wait_ge(s_const, 16)
            act.activation(ident_b[:, :], ident, ACT.Copy).then_inc(s_cb, 1)
            act.activation(mask_b[:, :], cst[:, C_MASK:C_MASK + P], ACT.Copy).then_inc(s_cb, 1)
            act.activation(lower_b[:, :], cst[:, C_LT:C_LT + P], ACT.Copy).then_inc(s_cb, 1)
            xt_head(0)
            w_head(1)
            w_head(2)
            swap(0, 2, 0)
            swap(0, 2, 1)
            qk_head(0, 0, 0)
            swap(2, 4, 0)
            qk_head(0, 0, 1)
            swap(2, 4, 1)
            v_head(6, 0)
            v_head(7, 1)
            qk_head(2, 1, 0)
            for m in range(2, 2 * NI):
                v_head(6 + m, m)
                if m == 5:
                    qk_head(2, 1, 1)
            batch(0)
            with act.Fori(1, B - 1) as b:
                batch(b)
            batch(B - 1, last=True)
            gate_exp(B - 1)
            for e in range(3, E):
                w2_head(e)

            act.wait_ge(s_texp, 1)
            act.wait_ge(s_fsmall, 64)

            def tile(j, k):
                e = act.value_load(tile_exp[0:1, bass.ds(j, 1)], min_val=0, max_val=E - 1)
                for half in range(2):
                    act.wait_ge(s_h1, 2 * j + half + 1)
                    if not (isinstance(j, int) and j == 0):
                        act.wait_ge(s_hidl, 2 * j - 1 + half)
                    for c in range(4 * half, 4 * half + 4):
                        ins = act.activation(hid[:, c, :], FH[2 * (k % 2) + half][:, (c % 4) * P:(c % 4 + 1) * P],
                                             ACT.Relu, scale=1.0,
                                             bias=b1_col[:, bass.ds(e, 1), c:c + 1].rearrange("p a b -> p (a b)"))
                    ins.then_inc(s_hid, 1)
                for half in range(2):
                    act.wait_ge(s_hid, 2 * j + half + 1)
                    act.activation(hidh[:, k % 2, 4 * half:4 * half + 4, :], hid[:, 4 * half:4 * half + 4, :],
                                   ACT.Copy).then_inc(s_hidh, 1)

            tile(0, 0)
            tile(1, 1)
            tile(2, 2)
            with act.Fori(0, NS // 6 - 1) as it:
                for k in range(6):
                    tile(6 * it + 3 + k, 3 + k)
            for j in range(NS - 6, NS):
                tile(j, j)

        @block.tensor
        def _(pe):
            def mm3(out_ap, lh, ll, rh, rl, start, stop):
                pe.matmul(out_ap, ll, rh, start=start, stop=False)
                pe.matmul(out_ap, lh, rl, start=False, stop=False)
                return pe.matmul(out_ap, lh, rh, start=False, stop=stop)

            def pp_free(g):
                if not (isinstance(g, int) and g < 2):
                    pe.wait_ge(s_ppread, g - 1)

            def xt(b, g):
                pe.wait_ge(s_xh, b + 1)
                for c in range(KC):
                    pp_free(g + c)
                    for i in range(NI):
                        mm = pe.transpose(PP[c][:, i * P:(i + 1) * P], xh[:, i, c * P:(c + 1) * P], ident)
                    mm.then_inc(s_ppdone, 1)

            def unit_project(g, kind, head, new_batch=False):
                if new_batch:
                    pe.wait_ge(s_ppread, g)
                else:
                    pp_free(g)
                for c in range(KC):
                    mm = mm3(PP[kind][:, :], wh[:, kind, c, head * DH:(head + 1) * DH],
                             wl[:, kind, c, head * DH:(head + 1) * DH], xth[:, c, :], xtl[:, c, :],
                             c == 0, c == KC - 1)
                mm.then_inc(s_ppdone, 1)

            def v_project(g, m):
                pp_free(g)
                i, half = m // 2, m % 2
                for c in range(KC):
                    mm = mm3(PP[m % 2][:, :], xth[:, c, i * P:(i + 1) * P], xtl[:, c, i * P:(i + 1) * P],
                             wh[:, 2, c, half * 512:half * 512 + 512], wl[:, 2, c, half * 512:half * 512 + 512],
                             c == 0, c == KC - 1)
                mm.then_inc(s_ppdone, 1)

            def score(b, h, i):
                if i == 0:
                    pe.wait_ge(s_qkl, 16 * b + 2 * h + 2)
                n = 32 * b + 4 * h + i
                if not (isinstance(b, int) and n < 2):
                    pe.wait_ge(s_exp, n - 1)
                w = (i + 1) * P
                par = h % 4
                mm3(SB[i % 2][:, 0:w], qkh[:, par, 0, i * P:(i + 1) * P], qkl[:, par, 0, i * P:(i + 1) * P],
                    qkh[:, par, 1, 0:w], qkl[:, par, 1, 0:w], True, False)
                pe.matmul(SB[i % 2][:, i * P:w], ident_b[:, :], mask_b[:, :],
                          start=False, stop=True).then_inc(s_score, 1)

            def turn_probs(b, h, c):
                if c == 0:
                    pe.wait_ge(s_pscaled, 8 * b + h + 1)
                if not (isinstance(b, int) and b == 0 and h == 0):
                    pe.wait_ge(s_ptl, 24 * b + 3 * h + c - 2)
                for j in ((0,), (1,), (2, 3))[c]:
                    for i in range(j, NI):
                        o = TOFF[j] - CHUNK[c][0] + (i - j) * P
                        mm = pe.transpose(PT[c][:, o:o + P], prob[:, h % 2, POFF[i] + j * P:POFF[i] + (j + 1) * P],
                                          ident)
                mm.then_inc(s_ptdone, 1)

            def ob_free(n):
                if not (isinstance(n, int) and n == 0):
                    pe.wait_ge(s_obread, n)

            def attend(b, h):
                if h == 0:
                    pe.wait_ge(s_ppread, PPN(b))
                ob_free(obn(b) + h)
                for j in range(NI):
                    if j < 3:
                        pe.wait_ge(s_ptl, 24 * b + 3 * h + j + 1)
                    at = slice(TOFF[j], TOFF[j] + (NI - j) * P)
                    mm = mm3(OB[:, j * P:T], vh[:, j, h * P:(h + 1) * P], vl[:, j, h * P:(h + 1) * P],
                             pth[:, at], ptl[:, at], j == 0, j == NI - 1)
                mm.then_inc(s_obdone, 1)

            def out_project(b, g, i):
                if i == 0:
                    pe.wait_ge(s_obread, obn(b) + H)
                pp_free(g)
                for h in range(H):
                    mm = pe.matmul(PP[i % 2][:, 0:D], ot[:, h, i * P:(i + 1) * P], wo[:, h, :],
                                   start=(h == 0), stop=(h == H - 1))
                mm.then_inc(s_ppdone, 1)

            def xn_turn(b, n, c):
                if c == 0:
                    pe.wait_ge(s_xn, b + 1)
                ob_free(n)
                for i in range(NI):
                    mm = pe.transpose(OB[:, i * P:(i + 1) * P], xn[:, i, c * P:(c + 1) * P], ident)
                mm.then_inc(s_obdone, 1)

            def affinity(n):
                ob_free(n)
                for i in range(NI):
                    for c in range(KC):
                        mm = pe.matmul(OB[:, i * E:(i + 1) * E], xnt[:, c, i * P:(i + 1) * P], cent[:, c, :],
                                       start=(c == 0), stop=(c == KC - 1))
                mm.then_inc(s_obdone, 1)

            def batch(b, last=False):
                ob, pp = obn(b), PPN(b)
                for h in range(H + 1):
                    _, g, _ = unit_at(b, h)
                    unit = has_units(h, last)
                    head = h + 2 if h < 6 else h - 7
                    if h < H:
                        score(b, h, 0)
                    if h >= 2:
                        attend(b, h - 2)
                    if h < H:
                        score(b, h, 1)
                    if unit:
                        unit_project(g, 0, head, h == 7)
                    if h == 6 and not last:
                        xt(b + 1, g)
                    if h < H:
                        score(b, h, 2)
                    if h >= 1:
                        for c in range(3):
                            turn_probs(b, h - 1, c)
                    if unit:
                        unit_project(g + 1, 1, head)
                    if h < H:
                        score(b, h, 3)
                if not last:
                    v_project(pp + 18, 0)
                attend(b, H - 1)
                if not last:
                    v_project(pp + 19, 1)
                o0 = pp + (20 if not last else 12)
                for i in range(NI):
                    out_project(b, o0 + i, i)
                if last:
                    xn_turn(b, ob + 8, 0)
                    xn_turn(b, ob + 9, 1)
                    affinity(ob + 10)
                else:
                    for m in range(2, 2 * NI):
                        v_project(pp + 22 + m, m)
                        if m == 4:
                            xn_turn(b, ob + 8, 0)
                        if m == 5:
                            xn_turn(b, ob + 9, 1)
                        if m == 6:
                            affinity(ob + 10)

            pe.wait_ge(s_const, 16)
            xt(0, 0)
            pe.wait_ge(s_wrest[0], KC)
            unit_project(2, 0, 0, True)
            pe.wait_ge(s_wrest[1], KC)
            unit_project(3, 1, 0)
            unit_project(4, 0, 1)
            unit_project(5, 1, 1)
            pe.wait_ge(s_wrest[2], KC)
            for m in range(2 * NI):
                v_project(6 + m, m)
            pe.wait_ge(s_cb, 5)
            pe.wait_ge(s_wsmall, 32)
            batch(0)
            with pe.Fori(1, B - 1) as b:
                batch(b)
            batch(B - 1, last=True)

            pe.wait_ge(s_hot, B)
            oh = onehot[:, :, :].rearrange("p t e -> p (t e)")
            pe.matmul(SB[0][:, 0:NT * E], lower_b[:, :], oh, start=True, stop=True)
            pe.matmul(SB[1][:, 0:NT * E], ones_b[:, :], oh, start=True, stop=True).then_inc(s_count, 1)
            for t in range(NT):
                if t % 4 == 0:
                    pe.wait_ge(s_route, t // 4 + 1)
                mm = pe.matmul(PT[0][:, 0:2 * NS], hot_lo[:, t % 16, :],
                               hot_tok[:, t % 16, :, :].rearrange("p a n -> p (a n)"),
                               start=(t == 0), stop=(t == NT - 1))
                if t % 4 == 3:
                    mm.then_inc(s_routeb, 1)

            def turn_z(j, k, used):
                pe.wait_ge(s_gat[k % 6], 16 * used + 16)
                if not (isinstance(j, int) and j == 0):
                    pe.wait_ge(s_ht, j)
                for c in range(KC):
                    mm = pe.transpose(FZ[:, c * P:(c + 1) * P], row_in[:, k % 6, c * P:(c + 1) * P], ident)
                mm.then_inc(s_zt, 1)

            def up(j, k, used):
                pe.wait_ge(s_ht, j + 1)
                pe.wait_ge(s_w1[k % 3], 16 * used + 16)
                for half in range(2):
                    if not (isinstance(j, int) and j < 2):
                        pe.wait_ge(s_hid, 2 * j - 3 + half)
                    for c4 in range(4):
                        for c in range(KC):
                            at = c * F + (4 * half + c4) * P
                            mm = pe.matmul(FH[2 * (k % 2) + half][:, c4 * P:(c4 + 1) * P], w1r[:, k % 3, at:at + P],
                                           ht[:, k % 2, c, :], start=(c == 0), stop=(c == KC - 1))
                    mm.then_inc(s_h1, 1)

            def down(j, k, e):
                if not (isinstance(j, int) and j < 2):
                    pe.wait_ge(s_yb, j - 1)
                for c in range(FC):
                    if c % 4 == 0:
                        pe.wait_ge(s_hidl, 2 * j + 1 + c // 4)
                    w2h, w2l = (w2s[:, bass.ds(e, 1), part, c * D:(c + 1) * D].rearrange("p o d -> p (o d)")
                                for part in range(2))
                    mm = mm3(FY[k % 2][:, 0:D], hidh[:, k % 2, c, :], hidl[:, k % 2, c, :], w2h, w2l,
                             c == 0, c == FC - 1)
                mm.then_inc(s_y, 1)

            pe.wait_ge(s_texp, 1)

            def expert(j):
                return pe.value_load(tile_exp[0:1, bass.ds(j, 1)], min_val=0, max_val=E - 1)

            e0 = expert(0)
            turn_z(0, 0, 0)
            up(0, 0, 0)
            turn_z(1, 1, 0)
            pe.wait_ge(s_w2l[0], 5)
            pe.wait_ge(s_w2l[1], 3)

            def step(j, k, used, used1, e_j):
                up(j + 1, k + 1, used1)
                turn_z(j + 2, k + 2, used)
                down(j, k, e_j)
                return expert(j + 1)

            for j in range(3):
                e0 = step(j, j, (j + 2) // 6, (j + 1) // 3, e0)
            with pe.Fori(0, NS // 6 - 1) as it:
                e0 = expert(6 * it + 3)
                for k in range(6):
                    e0 = step(6 * it + 3 + k, 3 + k, it + (k + 5) // 6, 2 * it + (k + 4) // 3, e0)
            e0 = expert(NS - 6)
            for j in range(NS - 6, NS - 2):
                e0 = step(j, j, (j + 2) // 6, (j + 1) // 3, e0)
            up(NS - 1, NS - 1, (NS - 1) // 3)
            down(NS - 2, NS - 2, e0)
            down(NS - 1, NS - 1, expert(NS - 1))

        @block.vector
        def _(dve):
            def norm_stats(k, src, made):
                for i in range(NI):
                    ins = dve.bn_stats(stats[k][:, i, :], src[:, i, :])
                ins.then_inc(made, 1)

            def norm_aggr(k, own, n, made):
                dve.wait_ge(own, n)
                passed(dve)
                for i in range(NI):
                    ins = dve.bn_aggr(mv[k][:, i, :], stats[k][:, i, :])
                ins.then_inc(made, 1)

            def norm_apply(k, dst, src, rdy, n, made):
                dve.wait_ge(rdy, n)
                for i in range(NI):
                    ins = dve.tensor_scalar(dst[:, i, 0:D], src[:, i, :], mv[k][:, i, 0:1], rstd[k][:, i:i + 1],
                                            ALU.subtract, ALU.mult)
                ins.then_inc(made, 1)

            def ln_x_stats(b):
                dve.wait_ge(s_xa, 16 * (b + 1))
                norm_stats(0, xa, s_lnx)
                norm_aggr(0, s_lnx, b + 1, s_xmean)

            def ln_x(b, g):
                if g is not None:
                    dve.wait_ge(s_ppdone, g)
                norm_apply(0, xh, xa, s_xrstd, b + 1, s_xh)

            def xt_rest(b):
                for c in range(KC):
                    dve.wait_ge(s_xth, 2 * b + c + 1)
                    dve.tensor_tensor(xtl[:, c, :], PP[c][:, :], xth[:, c, :].bitcast(F32),
                                      ALU.subtract).then_inc(s_ppread, 1)

            def times_cos(n, kind):
                dve.wait_ge(s_swap, n + kind + 1)
                if not (isinstance(n, int) and n + kind < 2):
                    dve.wait_ge(s_qkl, n + kind - 1)
                dve.tensor_tensor(rope_c[:, kind, :], PP[kind][:, :], cst[:, C_COS:C_COS + T],
                                  ALU.mult).then_inc(s_ppread, 1)

            def k_products(n):
                times_cos(n, 1)
                dve.tensor_tensor(rope_s[:, 1, :], rope_s[:, 1, :], cst[:, C_SIN:C_SIN + T],
                                  ALU.mult).then_inc(s_kprod, 2)

            def v_rest(b, m):
                dve.wait_ge(s_vh, 8 * b + m + 1)
                at = slice((m % 2) * 512, (m % 2) * 512 + 512)
                dve.tensor_tensor(vl[:, m // 2, at], PP[m % 2][:, :], vh[:, m // 2, at].bitcast(F32),
                                  ALU.subtract).then_inc(s_ppread, 1)

            def row_max(b, h, i):
                n = 32 * b + 4 * h + i
                dve.wait_ge(s_score, n + 1)
                dve.tensor_reduce(negmax[:, h % 2, i:i + 1], SB[i % 2][:, 0:(i + 1) * P], AX.X, ALU.max,
                                  negate=True).then_inc(s_max, 1)

            def scale_probs(b, h):
                dve.wait_ge(s_exp, 32 * b + 4 * h + 4)
                dve.reciprocal(rdenom[:, h % 2, :], denom[:, h % 2, :]).then_inc(s_rden, 1)
                dve.wait_ge(s_rden, 8 * b + h + 1)
                for i in range(NI):
                    p_i = prob[:, h % 2, POFF[i]:POFF[i] + (i + 1) * P]
                    ins = dve.tensor_scalar(p_i, p_i, rdenom[:, h % 2, i:i + 1], None, ALU.mult)
                ins.then_inc(s_pscaled, 1)

            def pt_rest(b, h, c):
                dve.wait_ge(s_pth, 24 * b + 3 * h + c + 1)
                lo, w = CHUNK[c]
                dve.tensor_tensor(ptl[:, lo:lo + w], PT[c][:, 0:w], pth[:, lo:lo + w].bitcast(F32),
                                  ALU.subtract).then_inc(s_ptl, 1)

            def residual(b, g, i):
                if i == 0:
                    dve.wait_ge(s_xr, 16 * (b + 1))
                dve.wait_ge(s_ppdone, g + 1)
                dve.tensor_tensor(x1[:, i, :], PP[i % 2][:, 0:D], xr[:, i, :], ALU.add).then_inc(s_ppread, 1)

            def choose(b):
                passed(dve)
                for i in range(NI):
                    ins = dve.max(top[:, i, :], aff[:, i, :])
                ins.then_inc(s_top, 1)
                dve.wait_ge(s_top, b + 1)
                passed(dve)
                for i in range(NI):
                    ins = dve.max_index(topi[:, i, :], top[:, i, :], aff[:, i, :])
                ins.then_inc(s_topi, 1)
                dve.wait_ge(s_topi, b + 1)
                dve.tensor_copy(topf[:, :], topi[:, :, 0]).then_inc(s_topf, 1)
                dve.wait_ge(s_topf, b + 1)
                dve.tensor_tensor(onehot[:, bass.ds(NI * b, NI), :],
                                  cst[:, C_IOTA:C_IOTA + E].rearrange("p (o e) -> p o e", o=1).broadcast_to([P, NI, E]),
                                  topf[:, :].rearrange("p (i o) -> p i o", o=1).broadcast_to([P, NI, E]),
                                  ALU.is_equal).then_inc(s_hot, 1)

            def gate(b):
                dve.wait_ge(s_ea, b + 1)
                dve.tensor_scalar(ealpha1[:, :], ealpha[:, :], 1.0, None, ALU.add).then_inc(s_ea1, 1)
                dve.wait_ge(s_ea1, b + 1)
                dve.reciprocal(gates[:, :, 0], ealpha1[:, :]).then_inc(s_gate, 1)

            def between(b, h, first, last):
                if h == 1 and not last:
                    ln_x_stats(b + 1)
                if h == 2 and not first:
                    dve.wait_ge(s_obread, obn(b))
                    choose(b - 1)
                if h == 3 and not last:
                    ln_x(b + 1, PPN(b) - 16 if not first else 2)
                if h == 4 and not first:
                    gate(b - 1)

            def batch(b, first=False, last=False):
                pp = PPN(b)
                for h in range(H + 1):
                    n, g, _ = unit_at(b, h)
                    unit = has_units(h, last)
                    if h < H:
                        row_max(b, h, 0)
                        row_max(b, h, 1)
                    if h >= 1:
                        scale_probs(b, h - 1)
                    if h < H:
                        row_max(b, h, 2)
                    between(b, h, first, last)
                    if unit:
                        times_cos(n, 0)
                    if h == 6 and not last:
                        xt_rest(b + 1)
                    if h >= 1:
                        for c in range(3):
                            pt_rest(b, h - 1, c)
                    if h < H:
                        row_max(b, h, 3)
                    if unit:
                        k_products(n)
                if not last:
                    v_rest(b + 1, 0)
                    v_rest(b + 1, 1)
                if not first:
                    dve.wait_ge(s_rows, ROWS(b))
                o0 = pp + (20 if not last else 12)
                for i in range(NI):
                    residual(b, o0 + i, i)
                    dve.wait_ge(s_ppread, o0 + i + 1)
                    ins = dve.bn_stats(stats[1][:, i, :], x1[:, i, :])
                ins.then_inc(s_lnn, 1)
                norm_aggr(1, s_lnn, b + 1, s_nstat)
                if not last:
                    v_rest(b + 1, 2)
                norm_apply(1, xn, x1, s_nrstd, b + 1, s_xn)
                if not last:
                    v_rest(b + 1, 3)
                    v_rest(b + 1, 4)
                dve.wait_ge(s_xn, b + 1)
                norm_stats(2, xn, s_lnz)
                if not last:
                    v_rest(b + 1, 5)
                norm_aggr(2, s_lnz, b + 1, s_zstat)
                if not last:
                    v_rest(b + 1, 6)
                dve.wait_ge(s_obdone, obn(b) + 10)
                dve.wait_ge(s_skip, b + 1)
                norm_apply(2, xn, xn, s_zrstd, b + 1, s_z)
                if not last:
                    v_rest(b + 1, 7)

            s_lnx, s_lnn, s_lnz, s_topi, s_topf, s_ea1 = s_own

            ln_x_stats(0)
            ln_x(0, None)
            for c in range(KC):
                dve.wait_ge(s_whead, c + 1)
                dve.scalar_tensor_tensor(wl[:, 0, c, :], w_raw[:, 0, c, :], 1.0 / DH, wh[:, 0, c, :].bitcast(F32),
                                         ALU.mult, ALU.subtract).then_inc(s_wrest[0], 1)
            xt_rest(0)
            w_rest(dve, 1, [1])
            w_rest(dve, 2)
            dve.wait_ge(s_const, 16)
            for n in (0, 2):
                times_cos(n, 0)
                k_products(n)
            for m in range(2 * NI):
                v_rest(0, m)
            batch(0, first=True)
            with dve.Fori(1, B - 1) as b:
                batch(b)
            batch(B - 1, last=True)
            dve.wait_ge(s_obread, obn(B))
            choose(B - 1)
            gate(B - 1)

            rc = [0]

            def own(ins):
                rc[0] += 1
                ins.then_inc(s_dve, 1)
                dve.wait_ge(s_dve, rc[0])

            flat = lambda a: a[:, :, :].rearrange("p a b -> p (a b)")
            dve.wait_ge(s_count, 1)
            own(dve.tensor_copy(tot[:, :, :].rearrange("p e t -> p t e"),
                                SB[1][:, 0:NT * E].rearrange("p (t e) -> p t e", e=E)))
            own(dve.tensor_tensor_scan(flat(cum), ones_f[:, :], flat(tot), 0.0, ALU.mult, ALU.add))
            own(dve.tensor_copy(cnt[:, :], cum[:, :, NT - 1]))
            own(dve.tensor_tensor(adj2[:, 1:E], cnt[:, 1:E], cnt[:, 0:E - 1], ALU.subtract))
            own(dve.tensor_copy(adj2[:, 0:1], cnt[:, 0:1]))
            own(dve.tensor_scalar(cnt_i[:, :], adj2[:, :], float(P - 1), None, ALU.add))
            own(dve.tensor_scalar(tiles_i[:, :], cnt_i[:, :], 7, None, ALU.logical_shift_right))
            own(dve.tensor_copy(tiles_f[:, :], tiles_i[:, :]))
            own(dve.tensor_tensor_scan(tiles_cum[:, :], ones_f[:, 0:E], tiles_f[:, :], 0.0, ALU.mult, ALU.add))
            own(dve.tensor_tensor(adj[:, :], tiles_cum[:, :], tiles_f[:, :], ALU.subtract))
            own(dve.scalar_tensor_tensor(adj[:, :], adj[:, :], float(P), cnt[:, :], ALU.mult, ALU.subtract))
            own(dve.tensor_tensor(adj[:, :], adj[:, :], adj2[:, :], ALU.add))
            own(dve.tensor_tensor(flat(cum), flat(cum), flat(tot), ALU.subtract))
            own(dve.tensor_tensor(cum[:, :, :], cum[:, :, :],
                                  adj[:, :].rearrange("p (e o) -> p e o", o=1).broadcast_to([P, E, NT]), ALU.add))
            own(dve.tensor_tensor(pos[:, :, :], SB[0][:, 0:NT * E].rearrange("p (t e) -> p t e", e=E),
                                  cum[:, :, :].rearrange("p e t -> p t e"), ALU.add))
            own(dve.tensor_tensor(pos[:, :, :], pos[:, :, :], onehot[:, :, :], ALU.mult))
            own(dve.tensor_reduce(slot[:, :], pos[:, :, :], AX.X, ALU.add))
            own(dve.tensor_copy(slot_i[:, :], slot[:, :]))
            own(dve.tensor_scalar(hi_i[:, :], slot_i[:, :], 7, None, ALU.logical_shift_right))
            own(dve.tensor_scalar(lo_i[:, :], slot_i[:, :], P - 1, None, ALU.bitwise_and))
            own(dve.tensor_copy(slot_hi[:, :], hi_i[:, :]))
            own(dve.tensor_copy(slot_lo[:, :], lo_i[:, :]))
            own(dve.tensor_tensor(below[:, :, :],
                                  tiles_cum[:, :].rearrange("p (o e) -> p o e", o=1).broadcast_to([P, NS, E]),
                                  cst[:, C_IOTA:C_IOTA + NS].rearrange("p (j o) -> p j o", o=1).broadcast_to([P, NS, E]),
                                  ALU.is_le))
            own(dve.tensor_reduce(below_n[:, :], below[:, :, :], AX.X, ALU.add))
            dve.tensor_scalar(tile_exp[:, :], below_n[:, :], float(E - 1), None, ALU.min).then_inc(s_texp, 1)
            dve.wait_ge(s_texp, 1)

            def expert(j):
                return dve.value_load(tile_exp[0:1, bass.ds(j, 1)], min_val=0, max_val=E - 1)

            wide = lambda a, n: a.rearrange("p (t o) -> p t o", o=1).broadcast_to([P, 4, n])
            count = lambda n: cst[:, C_IOTA:C_IOTA + n].rearrange("p (o n) -> p o n", o=1).broadcast_to([P, 4, n])
            for g in range(NT // 4):
                ts = slice(4 * g, 4 * g + 4)
                k, k2 = slice(g % 4 * 4, g % 4 * 4 + 4), slice(g % 2 * 4, g % 2 * 4 + 4)
                if g >= 2:
                    dve.wait_ge(s_route, g - 1)
                if g >= 4:
                    dve.wait_ge(s_routeb, g - 3)
                dve.tensor_tensor(hot_tile[:, k2, :], count(NS), wide(slot_hi[:, ts], NS),
                                  ALU.is_equal).then_inc(s_hhi, 1)
                dve.tensor_tensor(hot_lo[:, k, :], count(P), wide(slot_lo[:, ts], P), ALU.is_equal)
                dve.wait_ge(s_hhi, g + 1)
                dve.tensor_scalar(hot_tok[:, k, 0, :], hot_tile[:, k2, :], cst[:, C_PART:C_PART + 1], None, ALU.mult)
                dve.tensor_tensor(hot_tok[:, k, 1, :], hot_tile[:, k2, :],
                                  wide(cst[:, C_TOK + 4 * g:C_TOK + 4 * g + 4], NS), ALU.mult).then_inc(s_route, 1)
            e0, e1 = expert(0), expert(1)
            dve.wait_ge(s_routeb, NT // 4)
            own(dve.tensor_scalar(tok_hi[:, :], PT[0][:, NS:2 * NS], float(P), float(B * T), ALU.mult, ALU.add))
            dve.tensor_tensor(slot_tok[:, :], PT[0][:, 0:NS], tok_hi[:, :], ALU.add).then_inc(s_idx, 1)

            w2_rest(dve, 1, 5)
            w2_rest(dve, 1, 6)
            dve.wait_ge(s_fsmall, 64)

            def affine(j, k, e):
                dve.wait_ge(s_zt, j + 1)
                for c in range(KC):
                    ins = dve.tensor_scalar(ht[:, k % 2, c, :], FZ[:, c * P:(c + 1) * P],
                                            g_col[:, bass.ds(e, 1), c:c + 1].rearrange("p a b -> p (a b)"),
                                            b_col[:, bass.ds(e, 1), c:c + 1].rearrange("p a b -> p (a b)"),
                                            ALU.mult, ALU.add)
                ins.then_inc(s_ht, 1)

            def hidden_rest(j, k):
                for half in range(2):
                    dve.wait_ge(s_hidh, 2 * j + half + 1)
                    at = slice(4 * half, 4 * half + 4)
                    dve.tensor_tensor(hidl[:, k % 2, at, :], hid[:, at, :], hidh[:, k % 2, at, :].bitcast(F32),
                                      ALU.subtract).then_inc(s_hidl, 1)

            def combine(j, k, e, again):
                dve.wait_ge(s_y, j + 1)
                dve.tensor_tensor(row_in[:, k % 6, 0:D], FY[k % 2][:, 0:D],
                                  b2_all[:, bass.ds(e, 1), :].rearrange("p o d -> p (o d)"),
                                  ALU.add).then_inc(s_yb, 1)
                if again is not None:
                    dve.wait_ge(s_sca[k % 3], 16 * again)
                dve.wait_ge(s_yb, j + 1)
                dve.scalar_tensor_tensor(row_out[:, k % 3, :], row_in[:, k % 6, 0:D], row_in[:, k % 6, 2 * D:2 * D + 1],
                                         row_in[:, k % 6, D:2 * D], ALU.mult, ALU.add).then_inc(s_comb, 1)

            affine(0, 0, e0)
            w2_rest(dve, 1, 7)
            affine(1, 1, e1)
            hidden_rest(0, 0)

            def step(j, k, again, left=3):
                if left > 2:
                    affine(j + 2, k + 2, expert(j + 2))
                if left > 1:
                    hidden_rest(j + 1, k + 1)
                combine(j, k, expert(j), again)

            for j in range(3):
                step(j, j, None)
            with dve.Fori(0, NS // 6 - 1) as it:
                for k in range(6):
                    step(6 * it + 3 + k, 3 + k, 2 * it + 1 + k // 3)
            for j in range(NS - 6, NS):
                step(j, j, j // 3, NS - j)


_INS = ["x", "w_q", "w_k", "w_v", "w_o", "cent_t", "ln_g", "ln_b", "w1_t", "b1", "w2_t", "b2", "consts"]


def constants():
    import numpy as np
    f = np.float32
    c = np.zeros((P, C_END), f)
    half = DH // 2
    freqs = np.power(f(10000.0), -(np.arange(half, dtype=f) / f(half))).astype(f)
    rad = (np.arange(T, dtype=f)[:, None] * freqs[None, :]).astype(f)
    cos, sin = np.cos(rad).astype(f), np.sin(rad).astype(f)
    d = np.arange(P) % half
    c[:, C_COS:C_COS + T] = cos.T[d]
    c[:, C_SIN:C_SIN + T] = np.where(np.arange(P)[:, None] < half, -sin.T[d], sin.T[d])
    c[:, C_IOTA:C_IOTA + P] = np.arange(P)[None, :]
    c[:, C_TOK:C_TOK + NT] = np.arange(NT)[None, :] - NT
    c[:, C_PART] = np.arange(P)
    c[:, C_ID:C_ID + P] = np.eye(P)
    p, n = np.arange(P)[:, None], np.arange(P)[None, :]
    c[:, C_MASK:C_MASK + P] = np.where(n > p, f(-1e30), f(0.0))
    c[:, C_LT:C_LT + P] = (p < n)
    return c


def kernel(**inputs):
    import numpy as np
    import concourse.bacc as bacc
    from concourse.bass_utils import run_bass_kernel_spmd

    g = {k[3:]: np.asarray(a) for k, a in inputs.items()}
    arrays = {
        "x": g["attn_x"], "w_q": g["attn_w_aq"].reshape(D, H * DH), "w_k": g["attn_w_ak"].reshape(D, H * DH),
        "w_v": g["attn_w_av"].reshape(D, H * DH), "w_o": g["attn_w_ao"].reshape(H * DH, D),
        "cent_t": g["ffn_centroids"].T, "ln_g": g["ffn_ln_g"], "ln_b": g["ffn_ln_b"],
        "w1_t": g["ffn_w1"].transpose(0, 2, 1), "b1": g["ffn_b1"],
        "w2_t": g["ffn_w2"].transpose(0, 2, 1), "b2": g["ffn_b2"], "consts": constants(),
    }
    arrays = {k: np.ascontiguousarray(a) for k, a in arrays.items()}
    nc = bacc.Bacc("TRN2", target_bir_lowering=False, num_devices=1)
    ins = [nc.dram_tensor(k, arrays[k].shape, F32, kind="ExternalInput").ap() for k in _INS]
    out = nc.dram_tensor("out", (B, T, D), F32, kind="ExternalOutput").ap()
    tok_rows = nc.dram_tensor("tok_rows", (B * T + 1, ROW), F32, kind="Internal").ap()
    build(nc, *ins, out, tok_rows)
    r = run_bass_kernel_spmd(nc, [arrays], core_ids=[0])
    return r.results[0]["out"]
```
